# Optimizing a Trainium2 kernel written in Bass

```python
import numpy as np
import jax
import jax.numpy as jnp

def _softmax(x, axis=-1):
    return jax.nn.softmax(x, axis=axis)

def _gelu(x):
    return jax.nn.gelu(x, approximate=True)

def _silu(x):
    return jax.nn.silu(x)

def _sigmoid(x):
    return jax.nn.sigmoid(x)

def _layernorm(x, axis=-1, eps=1e-05):
    m = jnp.mean(x, axis=axis, keepdims=True)
    v = jnp.var(x, axis=axis, keepdims=True)
    return (x - m) / jnp.sqrt(v + eps)

def _scatter_add(tgt, idx, src, axis=0):
    return tgt.at[idx].add(src)

def _segment_sum(src, seg, n):
    return jax.ops.segment_sum(src, seg, n)
kernel_name = 'mk_adaln_d1_jaxref_r8_c57417'

def setup_inputs(seed: int=0):
    np.random.seed(seed)
    _w = jnp.asarray

    def _L0_attn_setup():
        import jax, jax.numpy as jnp
        import numpy as np
        BLOCK = 32
        NUM_HEADS = 16
        HEAD_DIM = 128
        FP4_GRID = jnp.array([0.0, 0.5, 1.0, 1.5, 2.0, 3.0, 4.0, 6.0], dtype=jnp.float32)

        def quantize_to_mxfp4(w, block_size=BLOCK):
            D, F = w.shape
            blocks = w.reshape(D // block_size, block_size, F)
            amax = jnp.max(jnp.abs(blocks), axis=1)
            e = jnp.floor(jnp.log2(jnp.maximum(amax, 1e-12) / 6.0))
            scale = jnp.exp2(e)
            v = blocks / scale[:, None, :]
            idx = jnp.argmin(jnp.abs(jnp.abs(v)[..., None] - FP4_GRID), axis=-1)
            codes = jnp.sign(v) * FP4_GRID[idx]
            return (codes.reshape(D, F).astype(jnp.float32), scale.astype(jnp.float32))

        def _mxfp4_matmul(x, codes, scales, block_size=BLOCK):
            w = codes * jnp.repeat(scales, block_size, axis=0)
            return x @ w
        key = jax.random.key(seed)
        ks = jax.random.split(key, 9)
        B, S, D = (2, 256, 256)
        feat = NUM_HEADS * HEAD_DIM
        x = jax.random.normal(ks[0], (B, S, D), dtype=jnp.float32)

        def make_w(k, din, dout):
            w = jax.random.normal(k, (din, dout), dtype=jnp.float32) * (1.0 / np.sqrt(din))
            return quantize_to_mxfp4(w, BLOCK)
        wq_codes, wq_scales = make_w(ks[1], D, feat)
        wk_codes, wk_scales = make_w(ks[2], D, feat)
        wv_codes, wv_scales = make_w(ks[3], D, feat)
        wo_codes, wo_scales = make_w(ks[4], feat, D)
        bq = jnp.zeros((feat,), jnp.float32)
        bk = jnp.zeros((feat,), jnp.float32)
        bv = jnp.zeros((feat,), jnp.float32)
        bo = jnp.zeros((D,), jnp.float32)
        return {'x': x, 'wq_codes': wq_codes, 'wq_scales': wq_scales, 'bq': bq, 'wk_codes': wk_codes, 'wk_scales': wk_scales, 'bk': bk, 'wv_codes': wv_codes, 'wv_scales': wv_scales, 'bv': bv, 'wo_codes': wo_codes, 'wo_scales': wo_scales, 'bo': bo}
    _L0_attn_in = _L0_attn_setup()

    def _L0_ffn_setup():
        import jax, jax.numpy as jnp
        import numpy as np
        B_, S_, H_, O_ = (4, 256, 256, 256)
        E_, R_ = (8, 16)
        LORA_ALPHA = 16.0
        key = jax.random.key(seed)
        ks = jax.random.split(key, 5)
        x = jax.random.normal(ks[0], (B_, S_, H_), dtype=jnp.float32)
        W = jax.random.normal(ks[1], (O_, H_), dtype=jnp.float32) * 0.02
        gate_w = jax.random.normal(ks[2], (E_, H_), dtype=jnp.float32) * 0.02
        A = jax.random.normal(ks[3], (E_, R_, H_), dtype=jnp.float32) * 0.02
        B = jax.random.normal(ks[4], (E_, O_, R_), dtype=jnp.float32) * 0.02
        return {'x': x, 'W': W, 'gate_w': gate_w, 'A': A, 'B': B}
    _L0_ffn_in = _L0_ffn_setup()
    _L0_c = _w((lambda *s: np.random.randn(*s).astype(np.float32) * 0.05)(4, 256))
    _L0_wmod = _w((lambda *s: np.random.randn(*s).astype(np.float32) * 0.05)(256, 6 * 256) * 256 ** (-0.5))
    _d = {'L0_attn_x': _L0_attn_in['x'], 'L0_attn_wq_codes': _L0_attn_in['wq_codes'], 'L0_attn_wq_scales': _L0_attn_in['wq_scales'], 'L0_attn_bq': _L0_attn_in['bq'], 'L0_attn_wk_codes': _L0_attn_in['wk_codes'], 'L0_attn_wk_scales': _L0_attn_in['wk_scales'], 'L0_attn_bk': _L0_attn_in['bk'], 'L0_attn_wv_codes': _L0_attn_in['wv_codes'], 'L0_attn_wv_scales': _L0_attn_in['wv_scales'], 'L0_attn_bv': _L0_attn_in['bv'], 'L0_attn_wo_codes': _L0_attn_in['wo_codes'], 'L0_attn_wo_scales': _L0_attn_in['wo_scales'], 'L0_attn_bo': _L0_attn_in['bo'], 'L0_ffn_W': _L0_ffn_in['W'], 'L0_ffn_gate_w': _L0_ffn_in['gate_w'], 'L0_ffn_A': _L0_ffn_in['A'], 'L0_ffn_B': _L0_ffn_in['B'], 'L0_c': _L0_c, 'L0_wmod': _L0_wmod}
    _x0 = _d['L0_attn_x']
    _d['L0_attn_x'] = jax.random.normal(jax.random.fold_in(jax.random.key(seed), 1), (4, 512, 256), dtype=_x0.dtype)
    del _x0
    return _d

def reference(L0_attn_x, L0_attn_wq_codes, L0_attn_wq_scales, L0_attn_bq, L0_attn_wk_codes, L0_attn_wk_scales, L0_attn_bk, L0_attn_wv_codes, L0_attn_wv_scales, L0_attn_bv, L0_attn_wo_codes, L0_attn_wo_scales, L0_attn_bo, L0_ffn_W, L0_ffn_gate_w, L0_ffn_A, L0_ffn_B, L0_c, L0_wmod):

    def _L0_attn_ref(x, wq_codes, wq_scales, bq, wk_codes, wk_scales, bk, wv_codes, wv_scales, bv, wo_codes, wo_scales, bo):
        import jax, jax.numpy as jnp
        import numpy as np
        BLOCK = 32
        NUM_HEADS = 16
        HEAD_DIM = 128
        FP4_GRID = jnp.array([0.0, 0.5, 1.0, 1.5, 2.0, 3.0, 4.0, 6.0], dtype=jnp.float32)

        def quantize_to_mxfp4(w, block_size=BLOCK):
            D, F = w.shape
            blocks = w.reshape(D // block_size, block_size, F)
            amax = jnp.max(jnp.abs(blocks), axis=1)
            e = jnp.floor(jnp.log2(jnp.maximum(amax, 1e-12) / 6.0))
            scale = jnp.exp2(e)
            v = blocks / scale[:, None, :]
            idx = jnp.argmin(jnp.abs(jnp.abs(v)[..., None] - FP4_GRID), axis=-1)
            codes = jnp.sign(v) * FP4_GRID[idx]
            return (codes.reshape(D, F).astype(jnp.float32), scale.astype(jnp.float32))

        def _mxfp4_matmul(x, codes, scales, block_size=BLOCK):
            w = codes * jnp.repeat(scales, block_size, axis=0)
            return x @ w
        B, S, D = x.shape
        q = _mxfp4_matmul(x, wq_codes, wq_scales) + bq
        k = _mxfp4_matmul(x, wk_codes, wk_scales) + bk
        v = _mxfp4_matmul(x, wv_codes, wv_scales) + bv
        q = q.reshape(B, S, NUM_HEADS, HEAD_DIM)
        k = k.reshape(B, S, NUM_HEADS, HEAD_DIM)
        v = v.reshape(B, S, NUM_HEADS, HEAD_DIM)
        scores = jnp.einsum('bqhd,bkhd->bhqk', q, k) / jnp.sqrt(jnp.float32(HEAD_DIM))
        attn = jax.nn.softmax(scores, axis=-1)
        out = jnp.einsum('bhqk,bkhd->bqhd', attn, v).reshape(B, S, NUM_HEADS * HEAD_DIM)
        return _mxfp4_matmul(out, wo_codes, wo_scales) + bo

    def _L0_ffn_ref(x, W, gate_w, A, B):
        import jax, jax.numpy as jnp
        import numpy as np
        B_, S_, H_, O_ = (4, 256, 256, 256)
        E_, R_ = (8, 16)
        LORA_ALPHA = 16.0
        bsz, seq, hid = x.shape
        E = gate_w.shape[0]
        x_flat = x.reshape(-1, hid)
        out = x_flat @ W.T
        logits = x_flat @ gate_w.T
        probs = jax.nn.softmax(logits, axis=-1)
        topk_w, topk_idx = jax.lax.top_k(probs, 2)
        topk_w = topk_w / jnp.sum(topk_w, axis=-1, keepdims=True)
        onehot = jax.nn.one_hot(topk_idx, E, dtype=x.dtype)
        wmat = jnp.einsum('tk,tke->te', topk_w, onehot) * LORA_ALPHA
        h = jnp.einsum('th,erh->etr', x_flat, A)
        hw = h * wmat.T[:, :, None]
        lora = jnp.einsum('etr,eor->to', hw, B)
        return (out + lora).reshape(bsz, seq, -1)
    x = L0_attn_x
    mod = (_silu(L0_c) @ L0_wmod).reshape(L0_c.shape[0], 6, 1, -1)
    sa, ca, ga, sb, cb, gb = (mod[:, 0], mod[:, 1], mod[:, 2], mod[:, 3], mod[:, 4], mod[:, 5])
    ga = (2 * (ga >= 0) - 1) * jnp.maximum(jnp.abs(ga), 0.25)
    gb = (2 * (gb >= 0) - 1) * jnp.maximum(jnp.abs(gb), 0.25)
    h = _layernorm(x, axis=-1) * (1 + ca) + sa
    x = x + ga * _L0_attn_ref(h, L0_attn_wq_codes, L0_attn_wq_scales, L0_attn_bq, L0_attn_wk_codes, L0_attn_wk_scales, L0_attn_bk, L0_attn_wv_codes, L0_attn_wv_scales, L0_attn_bv, L0_attn_wo_codes, L0_attn_wo_scales, L0_attn_bo)
    h = _layernorm(x, axis=-1) * (1 + cb) + sb
    x = x + gb * _L0_ffn_ref(h, L0_ffn_W, L0_ffn_gate_w, L0_ffn_A, L0_ffn_B)
    return x

_drawn_inputs = setup_inputs


def setup_inputs(seed=0):
    import zlib

    import numpy as np

    out = dict(_drawn_inputs(seed))
    spreads = {'L0_attn_bq': (0.0, 0.8),
     'L0_attn_bk': (0.0, 2.0),
     'L0_attn_bv': (0.0, 1.65),
     'L0_attn_bo': (0.0, 2.0)}
    factors = {'L0_attn_wq_codes': 3.465,
     'L0_attn_wq_scales': 8.0,
     'L0_attn_wk_codes': 3.484,
     'L0_attn_wk_scales': 8.0,
     'L0_attn_wv_codes': 2.944,
     'L0_attn_wv_scales': 8.0,
     'L0_attn_wo_scales': 5.008,
     'L0_ffn_W': 8.0,
     'L0_ffn_gate_w': 8.0,
     'L0_ffn_A': 8.0,
     'L0_ffn_B': 8.0}
    for name, (base, spread) in spreads.items():
        noise = np.random.default_rng([zlib.crc32(name.encode()), seed]).standard_normal(out[name].shape)
        drawn = base * np.exp(spread * noise) if base else spread * noise
        out[name] = jnp.asarray(drawn.astype(out[name].dtype))
    for name, factor in factors.items():
        out[name] = (out[name] * factor).astype(out[name].dtype)
    return out
```

```python
import concourse.bass as bass
from concourse import mybir
from contextlib import ExitStack


def bass_adaln_mxfp4_attention_moe_lora_kernel(
    nc: bass.Bass,
    x: bass.AP,
    wq_codes: bass.AP,
    wq_scales: bass.AP,
    bq: bass.AP,
    wk_codes: bass.AP,
    wk_scales: bass.AP,
    bk: bass.AP,
    wv_codes: bass.AP,
    wv_scales: bass.AP,
    bv: bass.AP,
    wo_codes: bass.AP,
    wo_scales: bass.AP,
    bo: bass.AP,
    ffn_w: bass.AP,
    gate_w: bass.AP,
    lora_a: bass.AP,
    lora_b: bass.AP,
    cond: bass.AP,
    wmod: bass.AP,
    out: bass.AP,
):
    f32 = mybir.dt.float32
    f32r = mybir.dt.float32r
    ALU = mybir.AluOpType
    ACT = mybir.ActivationFunctionType
    AX = mybir.AxisListType

    B, S, D = x.shape
    FEAT = wq_codes.shape[1]
    HD = 128
    P = 128
    PAIRS = FEAT // (2 * HD)
    PW = 2 * HD
    DC = D // P
    QT = S // P
    BLK = D // wq_scales.shape[0]
    NB = P // BLK
    SPB = 2
    SPP = SPB * B
    EXP, RANK = lora_a.shape[0], lora_a.shape[1]
    ER = EXP * RANK
    O = ffn_w.shape[0]
    LORA_ALPHA = 16.0
    EPS = 1e-5
    MODS = wmod.shape[1] // P
    SA, CA, GA, SB, CB, GB = (DC * i for i in range(6))
    NT = B * QT
    SCORE_SCALE = float(HD) ** -0.5
    assert D == 256 and S == 512 and ER == P and B == 4

    with ExitStack() as ctx:
        def sb(name, shape, dt=f32):
            return ctx.enter_context(nc.sbuf_tensor(name, shape, dt))

        def sem(name):
            return ctx.enter_context(nc.semaphore(name))

        ident = sb("ident", [P, P])
        x_nat = sb("x_nat", [P, NT, D])
        hT_hi = sb("hT_hi", [P, DC, B * S], f32r)
        hT_lo = sb("hT_lo", [P, DC, B * S], f32r)
        hT32 = sb("hT32", [P, 2, S])
        z = sb("z", [P, 2, QT, D])
        yT = sb("yT", [P, DC, B * S])
        wmod_sb = yT[:, :, :].rearrange("p c n -> p (c n)")[:, 0:DC * MODS * P].rearrange(
            "p (c n) -> p c n", c=DC)
        w_hi = {m: sb(f"w{m}_hi", [P, 2, PW], f32r) for m in "qkvo"}
        w_lo = {m: sb(f"w{m}_lo", [P, 2, PW], f32r) for m in "qkvo"}
        codes = {m: sb(f"w{m}_c", [P, 2, PW]) for m in "qkvo"}
        scales = {m: sb(f"w{m}_s", [P, 2, PW]) for m in "qkvo"}
        w32 = {m: sb(f"w{m}_32", [P, 2, PW]) for m in "qkvo"}
        q_hi, q_lo = sb("q_hi", [P, S], f32r), sb("q_lo", [P, S], f32r)
        k_hi, k_lo = sb("k_hi", [P, S], f32r), sb("k_lo", [P, S], f32r)
        v_hi = sb("v_hi", [P, 2, QT, PW], f32r)
        v_lo = sb("v_lo", [P, 2, QT, PW], f32r)
        v32 = sb("v32", [P, 2, PW])
        prob = sb("prob", [P, QT, S])
        pT_hi = sb("pT_hi", [P, 2, QT, S], f32r)
        pT_lo = sb("pT_lo", [P, 2, QT, S], f32r)
        o_hi, o_lo = sb("o_hi", [P, S], f32r), sb("o_lo", [P, S], f32r)
        neg_max = sb("neg_max", [P, QT])
        row_sum = sb("row_sum", [P, QT])
        inv_sum = sb("inv_sum", [P, QT])
        NH = FEAT // P
        VECS = 3 * NH + DC * B + DC
        vec_raw = sb("vec_raw", [VECS, P])
        vecT = sb("vecT", [P, VECS])
        bias = vecT[:, 0:3 * NH].rearrange("p (n h) -> p n h", n=3)
        cT = vecT[:, 3 * NH:3 * NH + DC * B].rearrange("p (c b) -> p c b", c=DC)
        bo_sb = vecT[:, 3 * NH + DC * B:VECS]
        bias_now = sb("bias_now", [P, 3, 2])
        c_exp = sb("c_exp", [P, DC, B])
        c_silu = sb("c_silu", [P, DC, B])
        modT = sb("modT", [P, MODS, B])
        mod_t = sb("mod_t", [P, 2, DC, B])
        gb_row = sb("gb_row", [P, B, D])
        stats = sb("stats", [P, 2, QT, 6])
        mv = sb("mv", [P, 2, QT, 2])
        rstd = sb("rstd", [P, 2, QT])
        var_eps = sb("var_eps", [P, 2, QT])
        minus_half = sb("minus_half", [P, 1])
        w_raw = prob[:, 0].rearrange("p (c d) -> p c d", c=O // P)
        a_raw = prob[:, 1, 0:D]
        g_raw = prob[0:EXP, 2, 0:D]
        b_raw = prob[:, 3, 0:O].rearrange("p (c e r) -> p c e r", c=O // P, e=EXP)
        wT = sb("wT", [P, DC, O])
        agT = sb("agT", [P, DC, ER + EXP])
        bT = sb("bT", [P, O])
        iota8 = sb("iota8", [P, QT, EXP])
        h2T = sb("h2T", [P, 2, DC, S])
        c_wide = h2T[:, 0].rearrange("p c (b q) -> p c b q", b=B)
        gb_t = h2T[:, :, :, :].rearrange("p i c s -> p (i c s)").rearrange("p (i b d) -> p i b d", i=2, b=B)
        logit = sb("logit", [P, QT, EXP])
        masked = sb("masked", [P, QT, EXP])
        cand = sb("cand", [P, QT, EXP])
        hot1 = sb("hot1", [P, QT, EXP])
        hot2 = sb("hot2", [P, QT, EXP])
        top = sb("top", [P, 8, QT])
        wmat = sb("wmat", [P, QT, EXP])
        hw = w32["q"][:, :, :].rearrange("p c (t n) -> p (c t) n", n=ER)
        hwT = w32["k"][:, :, :].rearrange("p c n -> p (c n)")
        res = hT32[:, :, :].rearrange("p i (t d) -> p i t d", t=2)

        def bank(name):
            return ctx.enter_context(nc.psum_tensor(name, [P, S], f32))

        score_ps = [bank("score0"), bank("score1")]
        tr_ps = [bank("tr0"), bank("tr1")]
        qv_ps, ky_ps, o_ps, y_ps = bank("qv"), bank("ky"), bank("o"), bank("y")

        ident_0, ident_ok, iota_ok, half_ok = (sem(n) for n in ("ident_0", "ident_ok", "iota_ok", "half_ok"))
        ld_vec, vec_tr, vec_ok, ld_wmod, ld_ffn = (sem(n) for n in ("ld_vec", "vec_tr", "vec_ok", "ld_wmod", "ld_ffn"))
        ld_x = [sem(f"ld_x{b}") for b in range(B)]
        ld_w = {m: sem(f"ld_w{m}") for m in "qkvo"}
        c_exped, silu_step, mod_mm, mod_ev, mod_ok, gbb_mm, gbb_ok = (
            sem(n) for n in ("c_exped", "silu_step", "mod_mm", "mod_ev", "mod_ok", "gbb_mm", "gbb_ok"))
        silu_ok = sem("silu_ok")
        bias_ok = sem("bias_ok")
        ffn_tr, ffn_ev = sem("ffn_tr"), sem("ffn_ev")
        ln_step, ln_var, ln_rstd, z_ok = (sem(n) for n in ("ln_step", "ln_var", "ln_rstd", "z_ok"))
        h_tr, h_ev, h_hi, h_lo = (sem(n) for n in ("h_tr", "h_ev", "h_hi", "h_lo"))
        w_prod = {m: sem(f"w{m}_prod") for m in "qkvo"}
        wq_scaled = sem("wq_scaled")
        w_hi_ok = {m: sem(f"w{m}_hi_ok") for m in "qkvo"}
        w_ok = {m: sem(f"w{m}_ok") for m in "qkvo"}
        q_mm, q_hi_ok, q_ok = sem("q_mm"), sem("q_hi_ok"), sem("q_ok")
        k_mm, k_hi_ok, k_ok = sem("k_mm"), sem("k_hi_ok"), sem("k_ok")
        v_mm, v_hi_ok, v32_ok, v_ok = sem("v_mm"), sem("v_hi_ok"), sem("v32_ok"), sem("v_ok")
        s_mm, max_ok, exp_ok, inv_ok, prob_ok = (sem(n) for n in ("s_mm", "max_ok", "exp_ok", "inv_ok", "prob_ok"))
        p_tr, p_hi_ok, p_ok = sem("p_tr"), sem("p_hi_ok"), sem("p_ok")
        o_mm, o_hi_ok, o_ok = sem("o_mm"), sem("o_hi_ok"), sem("o_ok")
        y_mm, y_ok = sem("y_mm"), sem("y_ok")
        yg_ok, x1_tr, x1_ok, z2_tr, z2_ev = (sem(n) for n in ("yg_ok", "x1_tr", "x1_ok", "z2_tr", "z2_ev"))
        ag_mm, router_step, margin_ok, e2_ok, f_mm = (sem(n) for n in ("ag_mm", "router_step", "margin_ok", "e2_ok", "f_mm"))
        hw_ok, hw_tr, hwT_ok, res_t, res_ok = (sem(n) for n in ("hw_ok", "hw_tr", "hwT_ok", "res_t", "res_ok"))
        stored = [sem("stored0"), sem("stored1")]

        CODES = dict(q=wq_codes, k=wk_codes, v=wv_codes, o=wo_codes)
        SCALES = dict(q=wq_scales, k=wk_scales, v=wv_scales, o=wo_scales)
        LDW = 16 * 3

        def batch_of(s):
            return (s % SPP) // SPB

        def tokens(b):
            return slice(b * S, (b + 1) * S)

        def ag_view(u):
            return (qv_ps, ky_ps)[u][:, 0:2 * (ER + EXP)].rearrange("p (t n) -> p t n", t=2)

        block = ctx.enter_context(nc.Block())

        @block.sync
        def _(sp):
            for i, vec in enumerate((bq, bk, bv)):
                sp.dma_start(vec_raw[i * NH:(i + 1) * NH, :], vec.rearrange("(h p) -> h p", p=P)).then_inc(ld_vec, 16)
            for c in range(DC):
                at = 3 * NH + c * B
                sp.dma_start(vec_raw[at:at + B, :], cond[:, c * P:(c + 1) * P]).then_inc(ld_vec, 16)
            sp.dma_start(vec_raw[VECS - DC:VECS, :], bo.rearrange("(c p) -> c p", p=P)).then_inc(ld_vec, 16)
            sp.dma_start(x_nat[:, 0:QT], x[0].rearrange("(t p) d -> p t d", p=P)).then_inc(ld_x[0], 16)
            sp.dma_start(wmod_sb, wmod.rearrange("(c p) n -> p c n", p=P)).then_inc(ld_wmod, 16)

            def load_weights(m, p):
                if m == "o":
                    rows = CODES[m].rearrange("(h p) d -> p h d", p=P)
                    sp.dma_start(codes[m][:, :, :], rows[:, bass.ds(2 * p, 2), :]).then_inc(ld_w[m], 16)
                    for j in range(2):
                        start = 2 * NB * D * p + j * NB * D
                        src = bass.AP(SCALES[m].tensor, start, [[D, NB], [0, BLK], [1, D]])
                        sp.dma_start(scales[m][:, j], src).then_inc(ld_w[m], 16)
                    return
                cols = CODES[m].rearrange("(c p) f -> p c f", p=P)
                sp.dma_start(codes[m][:, :, :], cols[:, :, bass.ds(PW * p, PW)]).then_inc(ld_w[m], 16)
                for c in range(DC):
                    start = PW * p + c * NB * FEAT
                    src = bass.AP(SCALES[m].tensor, start, [[FEAT, NB], [0, BLK], [1, PW]])
                    sp.dma_start(scales[m][:, c], src).then_inc(ld_w[m], 16)

            for m in "qkv":
                load_weights(m, 0)
            for b in range(1, B):
                sp.dma_start(x_nat[:, b * QT:(b + 1) * QT], x[b].rearrange("(t p) d -> p t d", p=P)).then_inc(ld_x[b], 16)
            load_weights("o", 0)
            sp.dma_start(w_raw[:, :, :], ffn_w.rearrange("(c p) d -> p c d", p=P)).then_inc(ld_ffn, 16)
            sp.dma_start(a_raw[:, :], lora_a.rearrange("e r d -> (e r) d")).then_inc(ld_ffn, 16)
            sp.dma_start(g_raw[:, :], gate_w).then_inc(ld_ffn, 16)
            for c in range(O // P):
                sp.dma_start(b_raw[:, c], lora_b[:, c * P:(c + 1) * P, :].rearrange("e p r -> p e r")).then_inc(ld_ffn, 16)

            def next_pair(p):
                for m in "vqk":
                    sp.wait_ge(w_ok[m], (1 if m == "v" else 2) * p)
                    load_weights(m, p)
                sp.wait_ge(w_ok["o"], 2 * p)
                load_weights("o", p)

            next_pair(1)
            with sp.Fori(2, PAIRS) as p:
                next_pair(p)

            for i in range(2 * B):
                sp.wait_ge(res_ok, i + 1)
                rows = out[i // 2, (i % 2) * 2 * P:(i % 2 + 1) * 2 * P, :].rearrange("(t p) d -> p t d", p=P)
                sp.dma_start(rows, res[:, i % 2]).then_inc(stored[i % 2], 16)
            for u in range(2):
                sp.wait_ge(stored[u], 16 * B)

        @block.gpsimd
        def _(pool):
            pool.memset(ident[:, :], 0.0).then_inc(ident_0, 1)
            pool.wait_ge(ident_0, 1)
            pool.affine_select(out=ident[:, :], in_=ident[:, :], compare_op=ALU.not_equal, fill=1.0,
                               base=0, pattern=[[-1, P]], channel_multiplier=1).then_inc(ident_ok, 1)
            pool.memset(minus_half[:, :], -0.5).then_inc(half_ok, 1)
            for e in range(EXP):
                pool.memset(iota8[:, :, e:e + 1], float(e)).then_inc(iota_ok, 1)
            pool.wait_ge(half_ok, 1)

            def inverse_std(i, par):
                pool.wait_ge(ln_var, i + 1)
                pool.tensor_tensor(rstd[:, par], var_eps[:, par], minus_half[:, :].to_broadcast([P, QT]),
                                   ALU.pow).then_inc(ln_rstd, 1)

            def product(m, p):
                pool.wait_ge(ld_w[m], LDW * (p + 1))
                if m == "q":
                    pool.wait_ge(wq_scaled, p + 1)
                if not (isinstance(p, int) and p == 0):
                    pool.wait_ge(w_ok[m], (1 if m == "v" else 2) * p)
                pool.tensor_tensor(w32[m][:, :, :], codes[m][:, :, :], scales[m][:, :, :], ALU.mult).then_inc(w_prod[m], 1)

            def parts(m, p, j):
                if m == "v":
                    cut, done = (slice(None), slice(None), slice(None)), p
                elif m == "o":
                    cut, done = (slice(None), j, slice(None)), 2 * p + j
                else:
                    cut, done = (slice(None), slice(None), slice(j * HD, (j + 1) * HD)), 2 * p + j
                pool.wait_ge(w_prod[m], p + 1)
                pool.tensor_tensor(w_hi[m][cut], codes[m][cut], scales[m][cut], ALU.mult).then_inc(w_hi_ok[m], 1)
                pool.wait_ge(w_hi_ok[m], done + 1)
                pool.tensor_tensor(w_lo[m][cut], w32[m][cut], w_hi[m][cut].bitcast(f32), ALU.subtract).then_inc(w_ok[m], 1)

            inverse_std(0, 0)
            for m in "qkv":
                product(m, 0)
                for j in range(1 if m == "v" else 2):
                    parts(m, 0, j)
            for b in range(1, B):
                inverse_std(b, b % 2)

            def v_low(count, par, half):
                pool.wait_ge(v_hi_ok, count)
                pool.wait_ge(v32_ok, count)
                pool.tensor_tensor(v_lo[:, par, 2 * half:2 * half + 2, :], v32[:, :, :],
                                   v_hi[:, par, 2 * half:2 * half + 2, :].bitcast(f32), ALU.subtract).then_inc(v_ok, 1)

            v_low(1, 0, 0)
            v_low(2, 0, 1)
            product("o", 0)

            def pair(p, last=False):
                for s in range(SPP):
                    n = SPP * p + s
                    for i in range(QT):
                        pool.wait_ge(inv_ok, QT * n + i + 1)
                        pool.tensor_tensor(prob[:, i], prob[:, i], inv_sum[:, i:i + 1].to_broadcast([P, S]),
                                           ALU.mult).then_inc(prob_ok, 1)
                    if s < 2:
                        if not (isinstance(p, int) and p == 0):
                            pool.wait_ge(y_mm, DC * (n - 1))
                        parts("o", p, s)
                    elif not last:
                        if s < 6:
                            product("vqko"[s - 2], p + 1)
                        else:
                            pool.wait_ge(k_mm, n + 1)
                            parts("q", p + 1, s - 6)
                            parts("k", p + 1, s - 6)
                    if not (last and s >= SPP - SPB):
                        v_low(n + 3, (batch_of(s) + 1) % 2, s % 2)
                    if s == 5 and not last:
                        parts("v", p + 1, 0)

            pair(0)
            with pool.Fori(1, PAIRS - 1) as p:
                pair(p)
            pair(PAIRS - 1, last=True)
            for b in range(B):
                inverse_std(B + b, b % 2)

        @block.scalar
        def _(act):
            act.wait_ge(vec_ok, 1)
            act.activation(c_exp[:, :, :], cT[:, :, :], ACT.Exp, scale=-1.0).then_inc(c_exped, 1)
            act.wait_ge(mod_mm, 1)
            act.activation(modT[:, :, :], y_ps[:, 0:MODS * B].rearrange("p (j b) -> p j b", b=B), ACT.Copy).then_inc(mod_ev, 1)

            def scale_codes(p):
                act.wait_ge(ld_w["q"], LDW * (p + 1))
                act.activation(codes["q"][:, :, :], codes["q"][:, :, :], ACT.Copy, scale=SCORE_SCALE).then_inc(wq_scaled, 1)

            scale_codes(0)
            act.wait_ge(vec_ok, 2)
            act.activation(bias_now[:, 0:2], bias[:, 0:2, 0:2], ACT.Copy).then_inc(bias_ok, 1)
            act.wait_ge(mod_ok, 1)
            for i in range(B * DC):
                b, c = i // DC, i % DC
                act.wait_ge(h_tr, i + 1)
                if i >= 2:
                    act.wait_ge(h_lo, i - 1)
                act.activation(hT32[:, i % 2], tr_ps[i % 2][:, :], ACT.Identity, bias=modT[:, SA + c, b:b + 1],
                               scale=modT[:, CA + c, b:b + 1]).then_inc(h_ev, 1)
            act.wait_ge(bias_ok, 1)

            def q_high(count, j):
                act.wait_ge(q_mm, count)
                act.activation(q_hi[:, :], qv_ps[:, :], ACT.Identity, bias=bias_now[:, 0, j:j + 1]).then_inc(q_hi_ok, 1)

            def k_high(count, j):
                act.wait_ge(k_mm, count)
                act.activation(k_hi[:, :], ky_ps[:, :], ACT.Identity, bias=bias_now[:, 1, j:j + 1]).then_inc(k_hi_ok, 1)

            def v_high(count, par, half):
                act.wait_ge(v_mm, count)
                ps = qv_ps[:, :].rearrange("p (t f) -> p t f", t=2)
                act.activation(v_hi[:, par, 2 * half:2 * half + 2, :], ps, ACT.Copy).then_inc(v_hi_ok, 1)
                if count_is_late(count):
                    act.wait_ge(v_ok, count - 1)
                act.activation(v32[:, :, :], ps, ACT.Copy).then_inc(v32_ok, 1)

            def count_is_late(count):
                return not (isinstance(count, int) and count == 1)

            q_high(1, 0)
            k_high(1, 0)
            v_high(1, 0, 0)
            act.wait_ge(ffn_tr, 1)
            act.activation(wT[:, :, :], score_ps[0][:, :].rearrange("p (c o) -> p c o", c=DC), ACT.Copy).then_inc(ffn_ev, 1)
            act.activation(agT[:, :, :], score_ps[1][:, 0:DC * (ER + EXP)].rearrange("p (c o) -> p c o", c=DC), ACT.Copy).then_inc(ffn_ev, 1)
            act.activation(bT[:, :], o_ps[:, 0:O], ACT.Copy).then_inc(ffn_ev, 1)
            v_high(2, 0, 1)

            def pair(p, first=False, last=False):
                for s in range(SPP):
                    n = SPP * p + s
                    start, end = first and s == 0, last and s == SPP - 1
                    for i in range(QT):
                        act.wait_ge(max_ok, QT * n + i + 1)
                        if not start:
                            act.wait_ge(p_tr, QT * (n - 1) + i + 1)
                        act.activation(prob[:, i], score_ps[i % 2][:, :], ACT.Exp, bias=neg_max[:, i:i + 1],
                                       accum_out=row_sum[:, i:i + 1]).then_inc(exp_ok, 1)
                    if not start:
                        act.wait_ge(o_mm, n)
                        act.activation(o_hi[:, :], o_ps[:, :], ACT.Identity,
                                       bias=bias_now[:, 2, (s - 1) % 2:(s - 1) % 2 + 1]).then_inc(o_hi_ok, 1)

                    def prob_high(i):
                        act.wait_ge(p_tr, QT * n + i + 1)
                        act.activation(pT_hi[:, s % 2, :, i * P:(i + 1) * P],
                                       tr_ps[i % 2][:, :].rearrange("p (k q) -> p k q", k=QT), ACT.Copy).then_inc(p_hi_ok, 1)

                    if s == 0 and not start:
                        act.wait_ge(o_hi_ok, n)
                    prob_high(0)
                    if s == 0:
                        act.activation(bias_now[:, 2], bias[:, 2, bass.ds(2 * p, 2)], ACT.Copy).then_inc(bias_ok, 1)
                        act.wait_ge(bias_ok, 2 * p + 2)
                    if not end:
                        q_high(n + 2, (s + 1) % 2)
                    prob_high(1)
                    if not end:
                        k_high(n + 2, (s + 1) % 2)
                    prob_high(2)
                    prob_high(3)
                    if not (last and s >= SPP - SPB):
                        if s == SPP - 2:
                            act.wait_ge(k_hi_ok, n + 2)
                        v_high(n + 3, (batch_of(s) + 1) % 2, s % 2)
                    if s == SPP - 2 and not last:
                        act.activation(bias_now[:, 0:2], bias[:, 0:2, bass.ds(2 * p + 2, 2)], ACT.Copy).then_inc(bias_ok, 1)
                        act.wait_ge(bias_ok, 2 * p + 3)
                    if s == 2 and not last:
                        scale_codes(p + 1)

            pair(0, first=True)
            with act.Fori(1, PAIRS - 1) as p:
                pair(p)
            pair(PAIRS - 1, last=True)

            act.wait_ge(o_mm, SPP * PAIRS)
            act.activation(o_hi[:, :], o_ps[:, :], ACT.Identity,
                           bias=bias_now[:, 2, 1:2]).then_inc(o_hi_ok, 1)

            for b in range(B):
                for c in range(DC):
                    act.wait_ge(z2_tr, DC * b + c + 1)
                    if b >= 2:
                        act.wait_ge(f_mm, 2 * (b - 1))
                    act.activation(h2T[:, b % 2, c], tr_ps[c][:, :], ACT.Identity, bias=modT[:, SB + c, b:b + 1],
                                   scale=modT[:, CB + c, b:b + 1]).then_inc(z2_ev, 1)
                act.wait_ge(margin_ok, b + 1)
                act.activation(top[:, 4], top[:, 3], ACT.Exp).then_inc(e2_ok, 1)
                act.wait_ge(hw_tr, b + 1)
                act.activation(hwT[:, :], score_ps[0][:, :], ACT.Copy).then_inc(hwT_ok, 1)

        @block.vector
        def _(dve):
            dve.wait_ge(vec_tr, 1)
            dve.tensor_copy(vecT[:, NH:VECS], o_ps[:, NH:VECS]).then_inc(vec_ok, 1)
            dve.tensor_scalar(vecT[:, 0:NH], o_ps[:, 0:NH], SCORE_SCALE, None, ALU.mult).then_inc(vec_ok, 1)
            dve.wait_ge(c_exped, 1)
            dve.tensor_scalar(c_exp[:, :, :], c_exp[:, :, :], 1.0, None, ALU.add).then_inc(silu_step, 1)
            dve.wait_ge(silu_step, 1)
            dve.reciprocal(c_exp[:, :, :], c_exp[:, :, :]).then_inc(silu_step, 1)
            dve.wait_ge(silu_step, 2)
            dve.tensor_tensor(c_silu[:, :, :], c_exp[:, :, :], cT[:, :, :], ALU.mult).then_inc(silu_ok, 1)
            dve.wait_ge(silu_ok, 1)
            dve.tensor_copy(c_wide[:, :, :, :].rearrange("p c b q -> p (c b) q"),
                            c_silu[:, :, :].rearrange("p c b -> p (c b)").unsqueeze(2).to_broadcast([P, DC * B, P])).then_inc(silu_ok, 1)

            steps = [0]

            def link(ins):
                steps[0] += 1
                ins.then_inc(ln_step, 1)
                dve.wait_ge(ln_step, steps[0])

            def normalise(i, b, par):
                for t in range(QT):
                    dve.bn_stats(stats[:, par, t], x_nat[:, b * QT + t]).then_inc(ln_step, 1)
                steps[0] += QT
                dve.wait_ge(ln_step, steps[0])
                for t in range(QT):
                    dve.bn_aggr(mv[:, par, t], stats[:, par, t]).then_inc(ln_step, 1)
                steps[0] += QT
                dve.wait_ge(ln_step, steps[0])
                dve.tensor_scalar(var_eps[:, par], mv[:, par, :, 1], EPS, None, ALU.add).then_inc(ln_var, 1)
                dve.wait_ge(ln_rstd, i + 1)
                for t in range(QT):
                    dve.tensor_scalar(z[:, par, t], x_nat[:, b * QT + t], mv[:, par, t, 0:1], rstd[:, par, t:t + 1],
                                      ALU.subtract, ALU.mult).then_inc(z_ok, 1)

            def h_parts(i):
                b, c = i // DC, i % DC
                dve.wait_ge(h_ev, i + 1)
                dve.tensor_copy(hT_hi[:, c, tokens(b)], hT32[:, i % 2]).then_inc(h_hi, 1)
                dve.wait_ge(h_hi, i + 1)
                dve.tensor_tensor(hT_lo[:, c, tokens(b)], hT32[:, i % 2], hT_hi[:, c, tokens(b)].bitcast(f32),
                                  ALU.subtract).then_inc(h_lo, 1)

            def magnitude_guard(dst, src, tmp, done):
                link(dve.tensor_scalar(tmp[0], src, -1.0, None, ALU.mult))
                link(dve.scalar_tensor_tensor(out=tmp[0], in0=tmp[0], scalar=0.25, in1=src, op0=ALU.max, op1=ALU.max))
                link(dve.tensor_scalar(tmp[1], src, 0.0, 2.0, ALU.is_ge, ALU.mult))
                dve.scalar_tensor_tensor(out=dst, in0=tmp[1], scalar=-1.0, in1=tmp[0], op0=ALU.add,
                                         op1=ALU.mult).then_inc(done, 1)

            dve.wait_ge(ld_x[0], 16)
            normalise(0, 0, 0)
            dve.wait_ge(mod_ev, 1)
            for k in (CA, CB):
                link(dve.tensor_scalar(modT[:, k:k + DC], modT[:, k:k + DC], 1.0, None, ALU.add))
            magnitude_guard(modT[:, GA:GA + DC], modT[:, GA:GA + DC], [mod_t[:, i] for i in range(2)], mod_ok)
            h_parts(0)
            h_parts(1)
            dve.wait_ge(gbb_mm, 1)
            link(dve.tensor_copy(gb_row[:, 0:2], qv_ps[:, :].rearrange("p (b d) -> p b d", b=2)))
            link(dve.tensor_copy(gb_row[:, 2:4], ky_ps[:, :].rearrange("p (b d) -> p b d", b=2)))
            magnitude_guard(gb_row[:, :, :], gb_row[:, :, :], [gb_t[:, i] for i in range(2)], gbb_ok)
            for b in range(1, B):
                dve.wait_ge(ld_x[b], 16)
                if b >= 2:
                    dve.wait_ge(h_tr, DC * (b - 1))
                normalise(b, b, b % 2)
                h_parts(DC * b)
                h_parts(DC * b + 1)

            def q_low(count, head):
                dve.wait_ge(q_hi_ok, count)
                dve.scalar_tensor_tensor(out=q_lo[:, :], in0=qv_ps[:, :], scalar=bias[:, 0, head], in1=q_hi[:, :].bitcast(f32),
                                         op0=ALU.add, op1=ALU.subtract).then_inc(q_ok, 1)

            def k_low(count, head):
                dve.wait_ge(k_hi_ok, count)
                dve.scalar_tensor_tensor(out=k_lo[:, :], in0=ky_ps[:, :], scalar=bias[:, 1, head], in1=k_hi[:, :].bitcast(f32),
                                         op0=ALU.add, op1=ALU.subtract).then_inc(k_ok, 1)

            def o_low(count, head):
                dve.wait_ge(o_hi_ok, count)
                dve.scalar_tensor_tensor(out=o_lo[:, :], in0=o_ps[:, :], scalar=bias[:, 2, head], in1=o_hi[:, :].bitcast(f32),
                                         op0=ALU.add, op1=ALU.subtract).then_inc(o_ok, 1)

            def y_add(count, b, c, fresh):
                ps = (y_ps, ky_ps)[c]
                dve.wait_ge(y_mm, count)
                if fresh:
                    dve.tensor_copy(yT[:, c, tokens(b)], ps[:, :]).then_inc(y_ok, 1)
                else:
                    dve.tensor_tensor(yT[:, c, tokens(b)], ps[:, :], yT[:, c, tokens(b)], ALU.add).then_inc(y_ok, 1)

            q_low(1, slice(0, 1))
            k_low(1, slice(0, 1))

            def head_slice(p, s):
                if s < 0:
                    h = 2 * p - 1
                elif s >= SPP:
                    h = 2 * p + 2
                else:
                    h = 2 * p + s % 2
                return bass.ds(h, 1)

            def pair(p, first=False, last=False):
                for s in range(SPP):
                    n = SPP * p + s
                    start, end = first and s == 0, last and s == SPP - 1

                    def maximum(i):
                        dve.wait_ge(s_mm, QT * n + i + 1)
                        dve.tensor_reduce(neg_max[:, i:i + 1], score_ps[i % 2][:, :], AX.X, ALU.max,
                                          negate=True).then_inc(max_ok, 1)

                    def inverse(i):
                        dve.wait_ge(exp_ok, QT * n + i + 1)
                        dve.reciprocal(inv_sum[:, i:i + 1], row_sum[:, i:i + 1]).then_inc(inv_ok, 1)

                    def prob_low(i):
                        dve.wait_ge(p_hi_ok, QT * n + i + 1)
                        dve.tensor_tensor(pT_lo[:, s % 2, :, i * P:(i + 1) * P],
                                          tr_ps[i % 2][:, :].rearrange("p (k q) -> p k q", k=QT),
                                          pT_hi[:, s % 2, :, i * P:(i + 1) * P].bitcast(f32), ALU.subtract).then_inc(p_ok, 1)

                    maximum(0)
                    maximum(1)
                    inverse(0)
                    maximum(2)
                    inverse(1)
                    maximum(3)
                    inverse(2)
                    inverse(3)
                    if not start:
                        o_low(n, head_slice(p, s - 1))
                    prob_low(0)
                    if not end:
                        q_low(n + 2, head_slice(p, s + 1))
                    prob_low(1)
                    if not end:
                        k_low(n + 2, head_slice(p, s + 1))
                    prob_low(2)
                    prob_low(3)
                    if not start:
                        for c in range(DC):
                            y_add(DC * (n - 1) + c + 1, batch_of(s - 1), c, first and s % 2 == 1)

            pair(0, first=True)
            with dve.Fori(1, PAIRS - 1) as p:
                pair(p)
            pair(PAIRS - 1, last=True)
            N = SPP * PAIRS
            o_low(N, slice(FEAT // P - 1, FEAT // P))
            for c in range(DC):
                y_add(DC * (N - 1) + c + 1, B - 1, c, False)

            dve.wait_ge(y_ok, DC * N)
            for b in range(B):
                for c in range(DC):
                    dve.tensor_scalar(yT[:, c, tokens(b)], yT[:, c, tokens(b)], bo_sb[:, c:c + 1],
                                      modT[:, GA + c, b:b + 1], ALU.add, ALU.mult).then_inc(yg_ok, 1)

            def ffn_input(b):
                for u in range(2):
                    dve.wait_ge(x1_tr, 2 * b + u + 1)
                    t = b * QT + 2 * u
                    dve.tensor_tensor(x_nat[:, t:t + 2], score_ps[1][:, :].rearrange("p (t d) -> p t d", t=2),
                                      x_nat[:, t:t + 2], ALU.add).then_inc(x1_ok, 1)
                dve.wait_ge(x1_ok, 2 * (b + 1))
                if b >= 2:
                    dve.wait_ge(z2_tr, DC * (b - 1))
                normalise(B + b, b, b % 2)

            chained = [0]

            def chain(ins):
                chained[0] += 1
                ins.then_inc(router_step, 1)
                dve.wait_ge(router_step, chained[0])

            def wide(v):
                return v.unsqueeze(2).to_broadcast([P, QT, EXP])

            def first_greatest(src, most, hot):
                chain(dve.tensor_reduce(most, src[:, :, :], AX.X, ALU.max))
                chain(dve.tensor_tensor(cand[:, :, :], src[:, :, :], wide(most), ALU.is_equal))
                chain(dve.scalar_tensor_tensor(out=cand[:, :, :], in0=cand[:, :, :], scalar=-float(EXP), in1=iota8[:, :, :],
                                               op0=ALU.mult, op1=ALU.add))
                chain(dve.tensor_reduce(top[:, 7], cand[:, :, :], AX.X, ALU.min))
                chain(dve.tensor_tensor(hot[:, :, :], cand[:, :, :], wide(top[:, 7]), ALU.is_equal))

            def router(b):
                dve.wait_ge(ag_mm, b + 1)
                for u in range(2):
                    chain(dve.tensor_copy(logit[:, 2 * u:2 * u + 2], ag_view(u)[:, :, ER:ER + EXP]))
                first_greatest(logit, top[:, 0], hot1)
                chain(dve.scalar_tensor_tensor(out=masked[:, :, :], in0=hot1[:, :, :], scalar=-3.0e38, in1=logit[:, :, :],
                                               op0=ALU.mult, op1=ALU.add))
                first_greatest(masked, top[:, 1], hot2)
                dve.tensor_tensor(top[:, 3], top[:, 1], top[:, 0], ALU.subtract).then_inc(margin_ok, 1)
                dve.wait_ge(e2_ok, b + 1)
                chain(dve.tensor_scalar(top[:, 5], top[:, 4], 1.0, None, ALU.add))
                chain(dve.reciprocal(top[:, 6], top[:, 5]))
                chain(dve.tensor_scalar(top[:, 5], top[:, 6], LORA_ALPHA, None, ALU.mult))
                chain(dve.tensor_tensor(top[:, 6], top[:, 5], top[:, 4], ALU.mult))
                chain(dve.tensor_tensor(hot1[:, :, :], hot1[:, :, :], wide(top[:, 5]), ALU.mult))
                chain(dve.tensor_tensor(hot2[:, :, :], hot2[:, :, :], wide(top[:, 6]), ALU.mult))
                chain(dve.tensor_tensor(wmat[:, :, :], hot1[:, :, :], hot2[:, :, :], ALU.add))
                if b:
                    dve.wait_ge(hw_tr, b)
                for u in range(2):
                    dve.tensor_tensor(hw[:, 2 * u:2 * u + 2].rearrange("p t (e r) -> p t e r", e=EXP),
                                      ag_view(u)[:, :, 0:ER].rearrange("p t (e r) -> p t e r", e=EXP),
                                      wmat[:, 2 * u:2 * u + 2].unsqueeze(3).to_broadcast([P, 2, EXP, RANK]),
                                      ALU.mult).then_inc(hw_ok, 1)

            def result(b):
                for u in range(2):
                    i = 2 * b + u
                    dve.wait_ge(f_mm, i + 1)
                    if b:
                        dve.wait_ge(stored[u], 16 * b)
                    dve.tensor_tensor(res[:, u], (o_ps, y_ps)[u][:, :].rearrange("p (t d) -> p t d", t=2),
                                      gb_row[:, b:b + 1].to_broadcast([P, 2, D]), ALU.mult).then_inc(res_t, 1)
                    dve.wait_ge(res_t, i + 1)
                    dve.tensor_tensor(res[:, u], res[:, u], x_nat[:, 2 * i:2 * i + 2], ALU.add).then_inc(res_ok, 1)

            dve.wait_ge(gbb_ok, 1)
            dve.wait_ge(iota_ok, EXP)
            ffn_input(0)
            for b in range(B):
                router(b)
                if b + 1 < B:
                    ffn_input(b + 1)
                result(b)

        @block.tensor
        def _(pe):
            def three(dst, a, b_, first, last, group_check=True):
                (a_hi, a_lo), (b_hi, b_lo) = a, b_
                pe.matmul(dst, a_hi, b_hi, start=first, stop=False)
                pe.matmul(dst, a_hi, b_lo, start=False, stop=False)
                return pe.matmul(dst, a_lo, b_hi, start=False, stop=last)

            pe.wait_ge(ident_ok, 1)
            pe.wait_ge(ld_vec, 16 * (3 + DC + 1))
            pe.transpose(o_ps[:, 0:VECS], vec_raw[:, :], ident[0:VECS, 0:VECS]).then_inc(vec_tr, 1)
            pe.wait_ge(ld_wmod, 16)
            pe.wait_ge(silu_ok, 2)
            for j in range(MODS):
                for c in range(DC):
                    ins = pe.matmul(y_ps[:, j * B:(j + 1) * B], wmod_sb[:, c, j * P:(j + 1) * P], c_silu[:, c],
                                    start=(c == 0), stop=(c == DC - 1))
            ins.then_inc(mod_mm, 1)

            def transpose_input(b):
                for c in range(DC):
                    i = DC * b + c
                    if c == 0:
                        pe.wait_ge(z_ok, QT * (b + 1))
                    if i >= 2:
                        pe.wait_ge(h_ev, i - 1)
                    for t in range(QT):
                        ins = pe.transpose(tr_ps[c][:, t * P:(t + 1) * P], z[:, b % 2, t, c * P:(c + 1) * P], ident[:, :])
                    ins.then_inc(h_tr, 1)

            transpose_input(0)
            for b in range(B):
                ps = (qv_ps, ky_ps)[b // 2]
                for c in range(DC):
                    ins = pe.matmul(ps[:, (b % 2) * D:(b % 2 + 1) * D], c_wide[:, c, b, :], wmod_sb[:, c, GB * P:GB * P + D],
                                    start=(c == 0), stop=(c == DC - 1))
            ins.then_inc(gbb_mm, 1)
            for b in range(1, B):
                transpose_input(b)

            def project(dst, m, j, b):
                for c in range(DC):
                    cut = (slice(None), c, slice(j * HD, (j + 1) * HD))
                    ins = three(dst[:, :], (w_hi[m][cut], w_lo[m][cut]),
                                (hT_hi[:, c, tokens(b)], hT_lo[:, c, tokens(b)]), c == 0, c == DC - 1)
                return ins

            def project_v(b, half):
                for t in range(2):
                    first = b * S + (2 * half + t) * P
                    for c in range(DC):
                        cut = (slice(None), c, slice(first, first + P))
                        ins = three(qv_ps[:, t * PW:(t + 1) * PW], (hT_hi[cut], hT_lo[cut]),
                                    (w_hi["v"][:, c], w_lo["v"][:, c]), c == 0, c == DC - 1)
                return ins

            pe.wait_ge(gbb_ok, 1)
            pe.wait_ge(h_lo, DC)
            pe.wait_ge(w_ok["q"], 1)
            project(qv_ps, "q", 0, 0).then_inc(q_mm, 1)
            pe.wait_ge(w_ok["k"], 1)
            project(ky_ps, "k", 0, 0).then_inc(k_mm, 1)
            pe.wait_ge(w_ok["v"], 1)
            pe.wait_ge(q_ok, 1)
            project_v(0, 0).then_inc(v_mm, 1)
            pe.wait_ge(ld_ffn, 16 * (3 + O // P))
            for c in range(DC):
                for r in range(O // P):
                    pe.transpose(score_ps[0][:, c * O + r * P:c * O + (r + 1) * P], w_raw[:, r, c * P:(c + 1) * P], ident[:, :])
                at = c * (ER + EXP)
                pe.transpose(score_ps[1][:, at:at + ER], a_raw[:, c * P:(c + 1) * P], ident[:, :])
                pe.transpose(score_ps[1][:, at + ER:at + ER + EXP], g_raw[:, c * P:(c + 1) * P], ident[0:EXP, 0:EXP])
            for r in range(O // P):
                ins = pe.transpose(o_ps[:, r * P:(r + 1) * P], b_raw[:, r].rearrange("p e r -> p (e r)"), ident[:, :])
            ins.then_inc(ffn_tr, 1)
            pe.wait_ge(v32_ok, 1)
            project_v(0, 1).then_inc(v_mm, 1)
            pe.wait_ge(ffn_ev, 3)

            def weighted(par_step, vpar, j, kt):
                cut = (slice(None), vpar, kt, slice(j * HD, (j + 1) * HD))
                return three(o_ps[:, :], (v_hi[cut], v_lo[cut]), (pT_hi[:, par_step, kt], pT_lo[:, par_step, kt]),
                             kt == 0, kt == QT - 1)

            def out_project(c, j):
                cut = (slice(None), j, slice(c * P, (c + 1) * P))
                return three((y_ps, ky_ps)[c][:, :], (w_hi["o"][cut], w_lo["o"][cut]), (o_hi[:, :], o_lo[:, :]), True, True)

            def pair(p, first=False, last=False):
                for s in range(SPP):
                    n = SPP * p + s
                    b = batch_of(s)
                    prev = (s - 1) % SPP
                    nxt = (s + 1) % SPP
                    start, end = first and s == 0, last and s == SPP - 1
                    early = first and s < 2
                    pe.wait_ge(q_ok, n + 1)
                    pe.wait_ge(k_ok, n + 1)
                    for i in range(QT):
                        if not (start and i < 2):
                            pe.wait_ge(exp_ok, QT * n + i - 1)
                        cut = (slice(None), slice(i * P, (i + 1) * P))
                        three(score_ps[i % 2][:, :], (q_hi[cut], q_lo[cut]), (k_hi[:, :], k_lo[:, :]),
                              True, True).then_inc(s_mm, 1)
                        if not start:
                            if i == 0:
                                pe.wait_ge(p_ok, QT * n)
                                pe.wait_ge(v_ok, n + s % 2)
                                if not early:
                                    pe.wait_ge(o_ok, n - 1)
                            ins = weighted((s - 1) % 2, batch_of(prev) % 2, prev % 2, i)
                            if i == QT - 1:
                                ins.then_inc(o_mm, 1)

                    def transpose_probs(i):
                        pe.wait_ge(prob_ok, QT * n + i + 1)
                        if not (start and i < 2):
                            pe.wait_ge(p_ok, QT * n + i - 1)
                        for kt in range(QT):
                            ins = pe.transpose(tr_ps[i % 2][:, kt * P:(kt + 1) * P], prob[:, i, kt * P:(kt + 1) * P], ident[:, :])
                        ins.then_inc(p_tr, 1)

                    transpose_probs(0)
                    if not end:
                        if first:
                            pe.wait_ge(h_lo, DC * (batch_of(nxt) + 1 if nxt else B))
                        if s >= SPP - 1 or s == 0:
                            pe.wait_ge(w_ok["q"], 2 * p + (3 if s else 2))
                        pe.wait_ge(v32_ok, n + 2)
                        project(qv_ps, "q", nxt % 2, batch_of(nxt)).then_inc(q_mm, 1)
                    transpose_probs(1)
                    if not end:
                        if s >= SPP - 1 or s == 0:
                            pe.wait_ge(w_ok["k"], 2 * p + (3 if s else 2))
                        if not early:
                            pe.wait_ge(y_ok, DC * (n - 1))
                        project(ky_ps, "k", nxt % 2, batch_of(nxt)).then_inc(k_mm, 1)
                    transpose_probs(2)
                    if not (last and s >= SPP - SPB):
                        if first:
                            pe.wait_ge(h_lo, DC * min(b + 2, B))
                        if s == SPP - SPB:
                            pe.wait_ge(w_ok["v"], p + 2)
                        pe.wait_ge(q_ok, n + 2)
                        project_v((b + 1) % B, s % 2).then_inc(v_mm, 1)
                    transpose_probs(3)
                    if not start:
                        pe.wait_ge(o_ok, n)
                        if s == 1 or s == 2:
                            pe.wait_ge(w_ok["o"], 2 * p + s)
                        if not early:
                            pe.wait_ge(y_ok, DC * (n - 1) - 1)
                        out_project(0, prev % 2).then_inc(y_mm, 1)
                        if not end:
                            pe.wait_ge(k_ok, n + 2)
                        else:
                            pe.wait_ge(y_ok, DC * (n - 1))
                        out_project(1, prev % 2).then_inc(y_mm, 1)

            pair(0, first=True)
            with pe.Fori(1, PAIRS - 1) as p:
                pair(p)
            pair(PAIRS - 1, last=True)

            N = SPP * PAIRS
            pe.wait_ge(p_ok, QT * N)
            pe.wait_ge(o_ok, N - 1)
            for kt in range(QT):
                ins = weighted((N - 1) % 2, (B - 1) % 2, 1, kt)
            ins.then_inc(o_mm, 1)
            pe.wait_ge(o_ok, N)
            pe.wait_ge(y_ok, DC * (N - 1))
            for c in range(DC):
                out_project(c, 1).then_inc(y_mm, 1)

            def rows_of_y(b):
                for u in range(2):
                    if 2 * b + u >= 1:
                        pe.wait_ge(x1_ok, 2 * b + u)
                    pe.wait_ge(yg_ok, DC * (b + 1))
                    for t in range(2):
                        for c in range(DC):
                            first = b * S + (2 * u + t) * P
                            ins = pe.transpose(score_ps[1][:, t * D + c * P:t * D + (c + 1) * P], yT[:, c, first:first + P], ident[:, :])
                    ins.then_inc(x1_tr, 1)

            rows_of_y(0)
            for b in range(B):
                pe.wait_ge(z_ok, QT * (B + b + 1))
                for c in range(DC):
                    if b:
                        pe.wait_ge(z2_ev, DC * (b - 1) + c + 1)
                    for t in range(QT):
                        ins = pe.transpose(tr_ps[c][:, t * P:(t + 1) * P], z[:, b % 2, t, c * P:(c + 1) * P], ident[:, :])
                    ins.then_inc(z2_tr, 1)
                pe.wait_ge(z2_ev, DC * (b + 1))
                if b:
                    pe.wait_ge(hw_ok, 2 * b)
                for t in range(QT):
                    for c in range(DC):
                        ins = pe.matmul(ag_view(t // 2)[:, t % 2], h2T[:, b % 2, c, t * P:(t + 1) * P], agT[:, c],
                                        start=(c == 0), stop=(c == DC - 1))
                ins.then_inc(ag_mm, 1)
                if b + 1 < B:
                    rows_of_y(b + 1)
                pe.wait_ge(hw_ok, 2 * (b + 1))
                if b:
                    pe.wait_ge(hwT_ok, b)
                for t in range(QT):
                    ins = pe.transpose(score_ps[0][:, t * P:(t + 1) * P], hw[:, t], ident[:, :])
                ins.then_inc(hw_tr, 1)
                pe.wait_ge(hwT_ok, b + 1)
                for u in range(2):
                    if b:
                        pe.wait_ge(res_t, 2 * (b - 1) + u + 1)
                    for t in range(2):
                        k = 2 * u + t
                        dst = (o_ps, y_ps)[u][:, t * D:(t + 1) * D]
                        for c in range(DC):
                            pe.matmul(dst, h2T[:, b % 2, c, k * P:(k + 1) * P], wT[:, c], start=(c == 0), stop=False)
                        ins = pe.matmul(dst, hwT[:, k * P:(k + 1) * P], bT[:, :], start=False, stop=True)
                    ins.then_inc(f_mm, 1)


_INS = ["L0_attn_x", "L0_attn_wq_codes", "L0_attn_wq_scales", "L0_attn_bq", "L0_attn_wk_codes", "L0_attn_wk_scales",
        "L0_attn_bk", "L0_attn_wv_codes", "L0_attn_wv_scales", "L0_attn_bv", "L0_attn_wo_codes", "L0_attn_wo_scales",
        "L0_attn_bo", "L0_ffn_W", "L0_ffn_gate_w", "L0_ffn_A", "L0_ffn_B", "L0_c", "L0_wmod"]
_OUTS = [((4, 512, 256), "float32")]


def kernel(**inputs):
    import numpy as _np
    import concourse.bacc as _bacc
    from concourse import mybir as _mybir
    from concourse.bass_utils import run_bass_kernel_spmd as _run

    nc = _bacc.Bacc("TRN2", target_bir_lowering=False, num_devices=1)
    arrays, args = {}, []
    for name in _INS:
        a = _np.ascontiguousarray(inputs[name])
        arrays[f"in_{name}_dram"] = a
        args.append(nc.dram_tensor(f"in_{name}_dram", a.shape, _mybir.dt.from_np(a.dtype), kind="ExternalInput").ap())
    for i, (shape, dtype) in enumerate(_OUTS):
        dt = _mybir.dt.from_np(_np.dtype(dtype))
        args.append(nc.dram_tensor(f"out_{i}_dram", shape, dt, kind="ExternalOutput").ap())
    bass_adaln_mxfp4_attention_moe_lora_kernel(nc, *args)
    r = _run(nc, [arrays], core_ids=[0])
    got = tuple(r.results[0][f"out_{i}_dram"] for i in range(len(_OUTS)))
    return got[0]
```

```python
import concourse.bass as bass
from concourse import mybir
from contextlib import ExitStack


def bass_adaln_mxfp4_attention_moe_lora_kernel(
    nc: bass.Bass,
    x: bass.AP,
    wq_codes: bass.AP,
    wq_scales: bass.AP,
    bq: bass.AP,
    wk_codes: bass.AP,
    wk_scales: bass.AP,
    bk: bass.AP,
    wv_codes: bass.AP,
    wv_scales: bass.AP,
    bv: bass.AP,
    wo_codes: bass.AP,
    wo_scales: bass.AP,
    bo: bass.AP,
    ffn_w: bass.AP,
    gate_w: bass.AP,
    lora_a: bass.AP,
    lora_b: bass.AP,
    cond: bass.AP,
    wmod: bass.AP,
    out: bass.AP,
):
    f32 = mybir.dt.float32
    f32r = mybir.dt.float32r
    ALU = mybir.AluOpType
    ACT = mybir.ActivationFunctionType
    AX = mybir.AxisListType

    B, S, D = x.shape
    FEAT = wq_codes.shape[1]
    HD = 128
    P = 128
    PAIRS = FEAT // (2 * HD)
    PW = 2 * HD
    DC = D // P
    QT = S // P
    BLK = D // wq_scales.shape[0]
    NB = P // BLK
    SPB = 2
    SPP = SPB * B
    EXP, RANK = lora_a.shape[0], lora_a.shape[1]
    ER = EXP * RANK
    O = ffn_w.shape[0]
    LORA_ALPHA = 16.0
    EPS = 1e-5
    MODS = wmod.shape[1] // P
    SA, CA, GA, SB, CB, GB = (DC * i for i in range(6))
    NT = B * QT
    SCORE_SCALE = float(HD) ** -0.5
    assert D == 256 and S == 512 and ER == P and B == 4

    with ExitStack() as ctx:
        def sb(name, shape, dt=f32):
            return ctx.enter_context(nc.sbuf_tensor(name, shape, dt))

        def sem(name):
            return ctx.enter_context(nc.semaphore(name))

        ident = sb("ident", [P, P])
        x_nat = sb("x_nat", [P, NT, D])
        hT_hi = sb("hT_hi", [P, DC, B * S], f32r)
        hT_lo = sb("hT_lo", [P, DC, B * S], f32r)
        hT32 = sb("hT32", [P, 2, S])
        z = sb("z", [P, 2, QT, D])
        yT = sb("yT", [P, DC, B * S])
        wmod_1 = yT[:, :, 0:(GA - SA) * P]
        w_hi = {m: sb(f"w{m}_hi", [P, 2, PW], f32r) for m in "qkvo"}
        w_lo = {m: sb(f"w{m}_lo", [P, 2, PW], f32r) for m in "qkvo"}
        stage = sb("stage", [P, 12, 2 * PW])

        def staged(i):
            return {m: stage[:, i + 3 * "qkvo".index(m)].rearrange("p (c n) -> p c n", c=2) for m in "qkvo"}

        codes, scales, w32 = staged(0), staged(1), staged(2)
        q_hi, q_lo = sb("q_hi", [P, S], f32r), sb("q_lo", [P, S], f32r)
        k_hi, k_lo = sb("k_hi", [P, S], f32r), sb("k_lo", [P, S], f32r)
        v_hi = sb("v_hi", [P, 2, QT, PW], f32r)
        v_lo = sb("v_lo", [P, 2, QT, PW], f32r)
        v32 = sb("v32", [P, 2, PW])
        prob = sb("prob", [P, QT, S])
        pT_hi = sb("pT_hi", [P, 2, QT, S], f32r)
        pT_lo = sb("pT_lo", [P, 2, QT, S], f32r)
        o_hi, o_lo = sb("o_hi", [P, S], f32r), sb("o_lo", [P, S], f32r)
        neg_max = sb("neg_max", [P, QT])
        row_sum = sb("row_sum", [P, QT])
        inv_sum = sb("inv_sum", [P, QT])
        NH = FEAT // P
        VECS = 3 * NH + DC
        c_raw = sb("c_raw", [B * DC, P])
        vec_raw = sb("vec_raw", [VECS, P])
        vecT = sb("vecT", [P, VECS])
        bias = vecT[:, 0:3 * NH].rearrange("p (n h) -> p n h", n=3)
        bo_sb = vecT[:, 3 * NH:VECS]
        bias_now = sb("bias_now", [P, 3, 2])
        c_exp = sb("c_exp", [P, B * DC])
        c_silu = sb("c_silu", [P, B * DC])
        modT = sb("modT", [P, MODS, B])
        gb_row = sb("gb_row", [P, B, D])
        stats = sb("stats", [P, 2, QT, 6])
        mv = sb("mv", [P, 2, QT, 2])
        rstd = sb("rstd", [P, 2, QT])
        var_eps = sb("var_eps", [P, 2, QT])
        minus_half = sb("minus_half", [P, 1])
        MOD2 = (MODS - GA) * P
        wmod_2 = stage[:, 0:4].rearrange("p i n -> p (i n)").rearrange("p (c n) -> p c n", c=DC)
        w_raw = stage[:, 4].rearrange("p (c d) -> p c d", c=O // P)
        a_raw = stage[:, 5, 0:D]
        g_raw = stage[0:EXP, 5, D:2 * D]
        b_raw = stage[:, 6, 0:O].rearrange("p (c e r) -> p c e r", c=O // P, e=EXP)
        mod_row = stage[0:B, 7:9].rearrange("b i n -> b (i n)")
        guard_t = stage[0:B, 9].rearrange("b (i n) -> b i n", i=2)
        pick = stage[0:B, 10].rearrange("k (b n) -> k b n", b=B)
        hw = stage[:, 4].rearrange("p (t n) -> p t n", n=ER)
        hwT = stage[:, 5]
        wT = sb("wT", [P, DC, O])
        agT = sb("agT", [P, DC, ER + EXP])
        bT = sb("bT", [P, O])
        iota8 = sb("iota8", [P, QT, EXP])
        h2T = sb("h2T", [P, 2, DC, S])
        logit = sb("logit", [P, QT, EXP])
        masked = sb("masked", [P, QT, EXP])
        cand = sb("cand", [P, QT, EXP])
        hot1 = sb("hot1", [P, QT, EXP])
        hot2 = sb("hot2", [P, QT, EXP])
        top = sb("top", [P, 8, QT])
        wmat = sb("wmat", [P, QT, EXP])
        res = hT32[:, :, :].rearrange("p i (t d) -> p i t d", t=2)

        def bank(name):
            return ctx.enter_context(nc.psum_tensor(name, [P, S], f32))

        score_ps = [bank("score0"), bank("score1")]
        tr_ps = [bank("tr0"), bank("tr1")]
        qv_ps, ky_ps, o_ps, y_ps = bank("qv"), bank("ky"), bank("o"), bank("y")

        ident_0, ident_ok, iota_ok, half_ok = (sem(n) for n in ("ident_0", "ident_ok", "iota_ok", "half_ok"))
        ld_c, c_tr, ld_vec, vec_tr, vec_ok, ld_wmod, ld_wmod2, ld_ffn = (
            sem(n) for n in ("ld_c", "c_tr", "ld_vec", "vec_tr", "vec_ok", "ld_wmod", "ld_wmod2", "ld_ffn"))
        ld_x = [sem(f"ld_x{b}") for b in range(B)]
        ld_w = {m: sem(f"ld_w{m}") for m in "qkvo"}
        c_exped, silu_step, mod_mm, mod_ok = (sem(n) for n in ("c_exped", "silu_step", "mod_mm", "mod_ok"))
        mod2_mm, mod2_ev, pick_ok, ga_ok, gb_ok, mod2_tr, gbb_mm, gbb_ok = (
            sem(n) for n in ("mod2_mm", "mod2_ev", "pick_ok", "ga_ok", "gb_ok", "mod2_tr", "gbb_mm", "gbb_ok"))
        silu_ok = sem("silu_ok")
        bias_ok = sem("bias_ok")
        ffn_tr, ffn_ev = sem("ffn_tr"), sem("ffn_ev")
        ln_step, ln_var, ln_rstd, z_ok = (sem(n) for n in ("ln_step", "ln_var", "ln_rstd", "z_ok"))
        h_tr, h_ev, h_hi, h_lo = (sem(n) for n in ("h_tr", "h_ev", "h_hi", "h_lo"))
        w_prod = {m: sem(f"w{m}_prod") for m in "qkvo"}
        wq_scaled = sem("wq_scaled")
        w_hi_ok = {m: sem(f"w{m}_hi_ok") for m in "qkvo"}
        w_ok = {m: sem(f"w{m}_ok") for m in "qkvo"}
        q_mm, q_hi_ok, q_ok = sem("q_mm"), sem("q_hi_ok"), sem("q_ok")
        k_mm, k_hi_ok, k_ok = sem("k_mm"), sem("k_hi_ok"), sem("k_ok")
        v_mm, v_hi_ok, v32_ok, v_ok = sem("v_mm"), sem("v_hi_ok"), sem("v32_ok"), sem("v_ok")
        s_mm, max_ok, exp_ok, inv_ok, prob_ok = (sem(n) for n in ("s_mm", "max_ok", "exp_ok", "inv_ok", "prob_ok"))
        p_tr, p_hi_ok, p_ok = sem("p_tr"), sem("p_hi_ok"), sem("p_ok")
        o_mm, o_hi_ok, o_ok = sem("o_mm"), sem("o_hi_ok"), sem("o_ok")
        y_zero, y_mm, y_ok = sem("y_zero"), sem("y_mm"), sem("y_ok")
        yg_ok, x1_tr, x1_ok, z2_tr, z2_ev = (sem(n) for n in ("yg_ok", "x1_tr", "x1_ok", "z2_tr", "z2_ev"))
        ag_mm, router_step, margin_ok, e2_ok, f_mm = (sem(n) for n in ("ag_mm", "router_step", "margin_ok", "e2_ok", "f_mm"))
        hw_ok, hw_tr, hwT_ok, res_t, res_ok = (sem(n) for n in ("hw_ok", "hw_tr", "hwT_ok", "res_t", "res_ok"))
        stored = [sem("stored0"), sem("stored1")]

        CODES = dict(q=wq_codes, k=wk_codes, v=wv_codes, o=wo_codes)
        SCALES = dict(q=wq_scales, k=wk_scales, v=wv_scales, o=wo_scales)
        LDW = 16 * 3

        INPUT_AT = {1: 2, 3: 3}

        def batch_of(s):
            return (s % SPP) // SPB

        def tokens(b):
            return slice(b * S, (b + 1) * S)

        def ag_view(u):
            return (qv_ps, ky_ps)[u][:, 0:2 * (ER + EXP)].rearrange("p (t n) -> p t n", t=2)

        block = ctx.enter_context(nc.Block())

        @block.sync
        def _(sp):
            sp.dma_start(c_raw[:, :], cond.rearrange("b (c p) -> (b c) p", p=P)).then_inc(ld_c, 16)
            sp.dma_start(x_nat[:, 0:QT], x[0].rearrange("(t p) d -> p t d", p=P)).then_inc(ld_x[0], 16)
            cols = wmod.rearrange("(c p) n -> p c n", p=P)
            sp.dma_start(wmod_1, cols[:, :, 0:GA * P]).then_inc(ld_wmod, 16)

            def load_weights(m, p):
                if m == "o":
                    rows = CODES[m].rearrange("(h p) d -> p h d", p=P)
                    sp.dma_start(codes[m][:, :, :], rows[:, bass.ds(2 * p, 2), :]).then_inc(ld_w[m], 16)
                    for j in range(2):
                        start = 2 * NB * D * p + j * NB * D
                        src = bass.AP(SCALES[m].tensor, start, [[D, NB], [0, BLK], [1, D]])
                        sp.dma_start(scales[m][:, j], src).then_inc(ld_w[m], 16)
                    return
                cols = CODES[m].rearrange("(c p) f -> p c f", p=P)
                sp.dma_start(codes[m][:, :, :], cols[:, :, bass.ds(PW * p, PW)]).then_inc(ld_w[m], 16)
                for c in range(DC):
                    start = PW * p + c * NB * FEAT
                    src = bass.AP(SCALES[m].tensor, start, [[FEAT, NB], [0, BLK], [1, PW]])
                    sp.dma_start(scales[m][:, c], src).then_inc(ld_w[m], 16)

            for m in "qkv":
                load_weights(m, 0)
            for i, vec in enumerate((bq, bk, bv, bo)):
                sp.dma_start(vec_raw[i * NH:min((i + 1) * NH, VECS), :], vec.rearrange("(h p) -> h p", p=P)).then_inc(ld_vec, 16)
            for b in range(1, B):
                sp.dma_start(x_nat[:, b * QT:(b + 1) * QT], x[b].rearrange("(t p) d -> p t d", p=P)).then_inc(ld_x[b], 16)
            load_weights("o", 0)

            def next_pair(p):
                for m in "vqk":
                    sp.wait_ge(w_ok[m], (1 if m == "v" else 2) * p)
                    load_weights(m, p)
                sp.wait_ge(w_ok["o"], 2 * p)
                load_weights("o", p)

            next_pair(1)
            with sp.Fori(2, PAIRS) as p:
                next_pair(p)

            for m in "vqk":
                sp.wait_ge(w_ok[m], (1 if m == "v" else 2) * PAIRS)
            sp.dma_start(wmod_2, cols[:, :, GA * P:MODS * P]).then_inc(ld_wmod2, 16)
            sp.dma_start(w_raw, ffn_w.rearrange("(c p) d -> p c d", p=P)).then_inc(ld_ffn, 16)
            sp.dma_start(a_raw, lora_a.rearrange("e r d -> (e r) d")).then_inc(ld_ffn, 16)
            sp.dma_start(g_raw, gate_w).then_inc(ld_ffn, 16)
            for c in range(O // P):
                sp.dma_start(b_raw[:, c], lora_b[:, c * P:(c + 1) * P, :].rearrange("e p r -> p e r")).then_inc(ld_ffn, 16)

            for i in range(2 * B):
                sp.wait_ge(res_ok, i + 1)
                rows = out[i // 2, (i % 2) * 2 * P:(i % 2 + 1) * 2 * P, :].rearrange("(t p) d -> p t d", p=P)
                sp.dma_start(rows, res[:, i % 2]).then_inc(stored[i % 2], 16)
            for u in range(2):
                sp.wait_ge(stored[u], 16 * B)

        @block.gpsimd
        def _(pool):
            pool.memset(ident[:, :], 0.0).then_inc(ident_0, 1)
            pool.wait_ge(ident_0, 1)
            pool.affine_select(out=ident[:, :], in_=ident[:, :], compare_op=ALU.not_equal, fill=1.0,
                               base=0, pattern=[[-1, P]], channel_multiplier=1).then_inc(ident_ok, 1)
            pool.memset(minus_half[:, :], -0.5).then_inc(half_ok, 1)
            for e in range(EXP):
                pool.memset(iota8[:, :, e:e + 1], float(e)).then_inc(iota_ok, 1)
            pool.memset(yT[:, DC - 1, tokens(B - 1)], 0.0).then_inc(y_zero, 1)
            pool.wait_ge(half_ok, 1)

            def inverse_std(i, par):
                pool.wait_ge(ln_var, i + 1)
                pool.tensor_tensor(rstd[:, par], var_eps[:, par], minus_half[:, :].to_broadcast([P, QT]),
                                   ALU.pow).then_inc(ln_rstd, 1)

            def product(m, p):
                pool.wait_ge(ld_w[m], LDW * (p + 1))
                if m == "q":
                    pool.wait_ge(wq_scaled, p + 1)
                if not (isinstance(p, int) and p == 0):
                    pool.wait_ge(w_ok[m], (1 if m == "v" else 2) * p)
                pool.tensor_tensor(w32[m][:, :, :], codes[m][:, :, :], scales[m][:, :, :], ALU.mult).then_inc(w_prod[m], 1)

            def parts(m, p, j):
                if m == "v":
                    cut, done = (slice(None), slice(None), slice(None)), p
                elif m == "o":
                    cut, done = (slice(None), j, slice(None)), 2 * p + j
                else:
                    cut, done = (slice(None), slice(None), slice(j * HD, (j + 1) * HD)), 2 * p + j
                pool.wait_ge(w_prod[m], p + 1)
                pool.tensor_tensor(w_hi[m][cut], codes[m][cut], scales[m][cut], ALU.mult).then_inc(w_hi_ok[m], 1)
                pool.wait_ge(w_hi_ok[m], done + 1)
                pool.tensor_tensor(w_lo[m][cut], w32[m][cut], w_hi[m][cut].bitcast(f32), ALU.subtract).then_inc(w_ok[m], 1)

            def input_lo(b):
                for c in range(DC):
                    pool.wait_ge(h_hi, DC * b + c + 1)
                    pool.tensor_tensor(hT_lo[:, c, tokens(b)], hT32[:, c], hT_hi[:, c, tokens(b)].bitcast(f32),
                                       ALU.subtract).then_inc(h_lo, 1)

            inverse_std(0, 0)
            for m in "qv":
                product(m, 0)
                for j in range(1 if m == "v" else 2):
                    parts(m, 0, j)
            inverse_std(1, 1)

            def v_low(count, par, half):
                pool.wait_ge(v_hi_ok, count)
                pool.wait_ge(v32_ok, count)
                pool.tensor_tensor(v_lo[:, par, 2 * half:2 * half + 2, :], v32[:, :, :],
                                   v_hi[:, par, 2 * half:2 * half + 2, :].bitcast(f32), ALU.subtract).then_inc(v_ok, 1)

            v_low(1, 0, 0)
            v_low(2, 0, 1)
            product("o", 0)

            def pair(p, first=False, last=False):
                for s in range(SPP):
                    n = SPP * p + s
                    for i in range(QT):
                        pool.wait_ge(inv_ok, QT * n + i + 1)
                        pool.tensor_tensor(prob[:, i], prob[:, i], inv_sum[:, i:i + 1].to_broadcast([P, S]),
                                           ALU.mult).then_inc(prob_ok, 1)
                    if first and s in INPUT_AT:
                        inverse_std(INPUT_AT[s], INPUT_AT[s] % 2)
                    if first and s - 1 in INPUT_AT:
                        input_lo(INPUT_AT[s - 1])
                    if s < 2:
                        if not first:
                            pool.wait_ge(y_mm, DC * (n - 1))
                        parts("o", p, s)
                    elif not last:
                        if s < 6:
                            product("vqko"[s - 2], p + 1)
                        else:
                            pool.wait_ge(k_mm, n + 1)
                            parts("q", p + 1, s - 6)
                            parts("k", p + 1, s - 6)
                    if not (last and s >= SPP - SPB):
                        v_low(n + 3, (batch_of(s) + 1) % 2, s % 2)
                    if s == 5 and not last:
                        parts("v", p + 1, 0)

            pair(0, first=True)
            with pool.Fori(1, PAIRS - 1) as p:
                pair(p)
            pair(PAIRS - 1, last=True)
            for b in range(B):
                inverse_std(B + b, b % 2)

        @block.scalar
        def _(act):
            act.wait_ge(c_tr, 1)
            act.activation(c_exp[:, :], o_ps[:, 0:B * DC], ACT.Exp, scale=-1.0).then_inc(c_exped, 1)

            def scale_codes(p):
                act.wait_ge(ld_w["q"], LDW * (p + 1))
                act.activation(codes["q"][:, :, :], codes["q"][:, :, :], ACT.Copy, scale=SCORE_SCALE).then_inc(wq_scaled, 1)

            scale_codes(0)
            act.wait_ge(mod_mm, 1)
            act.activation(modT[:, SA:SA + DC], ky_ps[:, 0:DC * B].rearrange("p (j b) -> p j b", b=B), ACT.Copy).then_inc(mod_ok, 1)
            act.activation(modT[:, CA:CA + DC], ky_ps[:, DC * B:2 * DC * B].rearrange("p (j b) -> p j b", b=B), ACT.Copy,
                           bias=1.0).then_inc(mod_ok, 1)
            act.wait_ge(mod_ok, 2)

            def input_high(b, c, banks):
                act.wait_ge(h_tr, DC * b + c + 1)
                if b:
                    act.wait_ge(h_lo, DC * (b - 1) + c + 1)
                for dst, done in ((hT32[:, c], h_ev), (hT_hi[:, c, tokens(b)], h_hi)):
                    act.activation(dst, banks[c][:, :], ACT.Identity, bias=modT[:, SA + c, b:b + 1],
                                   scale=modT[:, CA + c, b:b + 1]).then_inc(done, 1)

            for c in range(DC):
                input_high(0, c, tr_ps)
            act.wait_ge(vec_ok, 2)
            act.activation(bias_now[:, 0:2], bias[:, 0:2, 0:2], ACT.Copy).then_inc(bias_ok, 1)
            act.wait_ge(bias_ok, 1)

            def q_high(count, j):
                act.wait_ge(q_mm, count)
                act.activation(q_hi[:, :], qv_ps[:, :], ACT.Identity, bias=bias_now[:, 0, j:j + 1]).then_inc(q_hi_ok, 1)

            def k_high(count, j):
                act.wait_ge(k_mm, count)
                act.activation(k_hi[:, :], ky_ps[:, :], ACT.Identity, bias=bias_now[:, 1, j:j + 1]).then_inc(k_hi_ok, 1)

            def v_high(count, par, half):
                act.wait_ge(v_mm, count)
                ps = qv_ps[:, :].rearrange("p (t f) -> p t f", t=2)
                act.activation(v_hi[:, par, 2 * half:2 * half + 2, :], ps, ACT.Copy).then_inc(v_hi_ok, 1)
                if count_is_late(count):
                    act.wait_ge(v_ok, count - 1)
                act.activation(v32[:, :, :], ps, ACT.Copy).then_inc(v32_ok, 1)

            def count_is_late(count):
                return not (isinstance(count, int) and count == 1)

            q_high(1, 0)
            k_high(1, 0)
            v_high(1, 0, 0)
            v_high(2, 0, 1)

            def pair(p, first=False, last=False):
                for s in range(SPP):
                    n = SPP * p + s
                    start, end = first and s == 0, last and s == SPP - 1
                    for i in range(QT):
                        act.wait_ge(max_ok, QT * n + i + 1)
                        if not start:
                            act.wait_ge(p_tr, QT * (n - 1) + i + 1)
                        act.activation(prob[:, i], score_ps[i % 2][:, :], ACT.Exp, bias=neg_max[:, i:i + 1],
                                       accum_out=row_sum[:, i:i + 1]).then_inc(exp_ok, 1)
                        if first and s - 1 in INPUT_AT and i < DC:
                            input_high(INPUT_AT[s - 1], i, tr_ps)
                    if start:
                        for c in range(DC):
                            input_high(1, c, (o_ps, y_ps))
                    if not start:
                        act.wait_ge(o_mm, n)
                        act.activation(o_hi[:, :], o_ps[:, :], ACT.Identity,
                                       bias=bias_now[:, 2, (s - 1) % 2:(s - 1) % 2 + 1]).then_inc(o_hi_ok, 1)

                    def prob_high(i):
                        act.wait_ge(p_tr, QT * n + i + 1)
                        act.activation(pT_hi[:, s % 2, :, i * P:(i + 1) * P],
                                       tr_ps[i % 2][:, :].rearrange("p (k q) -> p k q", k=QT), ACT.Copy).then_inc(p_hi_ok, 1)

                    if s == 0 and not start:
                        act.wait_ge(o_hi_ok, n)
                    prob_high(0)
                    if s == 0:
                        act.activation(bias_now[:, 2], bias[:, 2, bass.ds(2 * p, 2)], ACT.Copy).then_inc(bias_ok, 1)
                        act.wait_ge(bias_ok, 2 * p + 2)
                    if not end:
                        q_high(n + 2, (s + 1) % 2)
                    prob_high(1)
                    if not end:
                        k_high(n + 2, (s + 1) % 2)
                    prob_high(2)
                    if end:
                        for i in range(2):
                            act.wait_ge(mod2_mm, i + 1)
                            act.activation(mod_row[:, i * S:(i + 1) * S], (qv_ps, ky_ps)[i][0:B, :], ACT.Copy).then_inc(mod2_ev, 1)
                    prob_high(3)
                    if not (last and s >= SPP - SPB):
                        if s == SPP - 2:
                            act.wait_ge(k_hi_ok, n + 2)
                        v_high(n + 3, (batch_of(s) + 1) % 2, s % 2)
                    if s == SPP - 2 and not last:
                        act.activation(bias_now[:, 0:2], bias[:, 0:2, bass.ds(2 * p + 2, 2)], ACT.Copy).then_inc(bias_ok, 1)
                        act.wait_ge(bias_ok, 2 * p + 3)
                    if s == 2 and not last:
                        scale_codes(p + 1)

            pair(0, first=True)
            with act.Fori(1, PAIRS - 1) as p:
                pair(p)
            pair(PAIRS - 1, last=True)

            act.wait_ge(mod2_tr, 1)
            for k, add in ((GA, 0.0), (SB, 0.0), (CB, 1.0)):
                at = (k - GA) * B
                act.activation(modT[:, k:k + DC], qv_ps[:, at:at + DC * B].rearrange("p (j b) -> p j b", b=B), ACT.Copy,
                               bias=add).then_inc(mod_ok, 1)
            for i in range(2):
                act.wait_ge(gbb_mm, i + 1)
                act.activation(gb_row[:, 2 * i:2 * i + 2], score_ps[i][:, :].rearrange("p (b d) -> p b d", b=2), ACT.Copy).then_inc(gbb_ok, 1)
            act.wait_ge(o_mm, SPP * PAIRS)
            act.activation(o_hi[:, :], o_ps[:, :], ACT.Identity,
                           bias=bias_now[:, 2, 1:2]).then_inc(o_hi_ok, 1)
            act.wait_ge(ffn_tr, 1)
            act.activation(wT[:, :, :], tr_ps[0][:, :].rearrange("p (c o) -> p c o", c=DC), ACT.Copy).then_inc(ffn_ev, 1)
            act.activation(agT[:, :, :], tr_ps[1][:, 0:DC * (ER + EXP)].rearrange("p (c o) -> p c o", c=DC), ACT.Copy).then_inc(ffn_ev, 1)
            act.activation(bT[:, :], qv_ps[:, 0:O], ACT.Copy).then_inc(ffn_ev, 1)
            act.wait_ge(mod_ok, 5)

            for b in range(B):
                for c in range(DC):
                    act.wait_ge(z2_tr, DC * b + c + 1)
                    if b >= 2:
                        act.wait_ge(f_mm, 2 * (b - 1))
                    act.activation(h2T[:, b % 2, c], tr_ps[c][:, :], ACT.Identity, bias=modT[:, SB + c, b:b + 1],
                                   scale=modT[:, CB + c, b:b + 1]).then_inc(z2_ev, 1)
                act.wait_ge(margin_ok, b + 1)
                act.activation(top[:, 4], top[:, 3], ACT.Exp).then_inc(e2_ok, 1)
                act.wait_ge(hw_tr, b + 1)
                act.activation(hwT[:, :], score_ps[0][:, :], ACT.Copy).then_inc(hwT_ok, 1)

        @block.vector
        def _(dve):
            dve.wait_ge(c_exped, 1)
            dve.tensor_scalar(c_exp[:, :], c_exp[:, :], 1.0, None, ALU.add).then_inc(silu_step, 1)
            dve.wait_ge(silu_step, 1)
            dve.reciprocal(c_exp[:, :], c_exp[:, :]).then_inc(silu_step, 1)
            dve.wait_ge(silu_step, 2)
            dve.tensor_tensor(c_silu[:, :], c_exp[:, :], o_ps[:, 0:B * DC], ALU.mult).then_inc(silu_ok, 1)

            steps = [0]

            def link(ins):
                steps[0] += 1
                ins.then_inc(ln_step, 1)
                dve.wait_ge(ln_step, steps[0])

            def statistics(b, par):
                for t in range(QT):
                    dve.bn_stats(stats[:, par, t], x_nat[:, b * QT + t]).then_inc(ln_step, 1)
                steps[0] += QT
                dve.wait_ge(ln_step, steps[0])
                for t in range(QT):
                    dve.bn_aggr(mv[:, par, t], stats[:, par, t]).then_inc(ln_step, 1)
                steps[0] += QT
                dve.wait_ge(ln_step, steps[0])
                dve.tensor_scalar(var_eps[:, par], mv[:, par, :, 1], EPS, None, ALU.add).then_inc(ln_var, 1)

            def normalise(i, b, par):
                dve.wait_ge(ln_rstd, i + 1)
                for t in range(QT):
                    dve.tensor_scalar(z[:, par, t], x_nat[:, b * QT + t], mv[:, par, t, 0:1], rstd[:, par, t:t + 1],
                                      ALU.subtract, ALU.mult).then_inc(z_ok, 1)

            def input_lo(b):
                for c in range(DC):
                    dve.wait_ge(h_hi, DC * b + c + 1)
                    dve.tensor_tensor(hT_lo[:, c, tokens(b)], hT32[:, c], hT_hi[:, c, tokens(b)].bitcast(f32),
                                      ALU.subtract).then_inc(h_lo, 1)

            def magnitude_guard(dst, src, tmp, done):
                link(dve.tensor_scalar(tmp[0], src, -1.0, None, ALU.mult))
                link(dve.scalar_tensor_tensor(out=tmp[0], in0=tmp[0], scalar=0.25, in1=src, op0=ALU.max, op1=ALU.max))
                link(dve.tensor_scalar(tmp[1], src, 0.0, 2.0, ALU.is_ge, ALU.mult))
                dve.scalar_tensor_tensor(out=dst, in0=tmp[1], scalar=-1.0, in1=tmp[0], op0=ALU.add,
                                         op1=ALU.mult).then_inc(done, 1)

            dve.wait_ge(ld_x[0], 16)
            statistics(0, 0)
            normalise(0, 0, 0)
            dve.wait_ge(ld_w["k"], LDW)
            wk = (codes["k"], scales["k"], w32["k"])
            dve.tensor_tensor(wk[2], wk[0], wk[1], ALU.mult).then_inc(w_prod["k"], 1)
            dve.tensor_tensor(w_hi["k"][:, :, :], wk[0], wk[1], ALU.mult).then_inc(w_hi_ok["k"], 2)
            dve.wait_ge(w_prod["k"], 1)
            dve.wait_ge(w_hi_ok["k"], 2)
            dve.tensor_tensor(w_lo["k"][:, :, :], wk[2], w_hi["k"][:, :, :].bitcast(f32), ALU.subtract).then_inc(w_ok["k"], 2)
            input_lo(0)
            dve.wait_ge(vec_tr, 1)
            dve.tensor_copy(vecT[:, NH:VECS], y_ps[:, NH:VECS]).then_inc(vec_ok, 1)
            dve.tensor_scalar(vecT[:, 0:NH], y_ps[:, 0:NH], SCORE_SCALE, None, ALU.mult).then_inc(vec_ok, 1)
            dve.wait_ge(vec_ok, 2)

            def q_low(count, head):
                dve.wait_ge(q_hi_ok, count)
                dve.scalar_tensor_tensor(out=q_lo[:, :], in0=qv_ps[:, :], scalar=bias[:, 0, head], in1=q_hi[:, :].bitcast(f32),
                                         op0=ALU.add, op1=ALU.subtract).then_inc(q_ok, 1)

            def k_low(count, head):
                dve.wait_ge(k_hi_ok, count)
                dve.scalar_tensor_tensor(out=k_lo[:, :], in0=ky_ps[:, :], scalar=bias[:, 1, head], in1=k_hi[:, :].bitcast(f32),
                                         op0=ALU.add, op1=ALU.subtract).then_inc(k_ok, 1)

            def o_low(count, head):
                dve.wait_ge(o_hi_ok, count)
                dve.scalar_tensor_tensor(out=o_lo[:, :], in0=o_ps[:, :], scalar=bias[:, 2, head], in1=o_hi[:, :].bitcast(f32),
                                         op0=ALU.add, op1=ALU.subtract).then_inc(o_ok, 1)

            def y_add(count, b, c, fresh):
                ps = (y_ps, ky_ps)[c]
                dve.wait_ge(y_mm, count)
                if fresh:
                    dve.tensor_copy(yT[:, c, tokens(b)], ps[:, :]).then_inc(y_ok, 1)
                else:
                    dve.tensor_tensor(yT[:, c, tokens(b)], ps[:, :], yT[:, c, tokens(b)], ALU.add).then_inc(y_ok, 1)

            q_low(1, slice(0, 1))
            k_low(1, slice(0, 1))

            def head_slice(p, s):
                if s < 0:
                    h = 2 * p - 1
                elif s >= SPP:
                    h = 2 * p + 2
                else:
                    h = 2 * p + s % 2
                return bass.ds(h, 1)

            def pair(p, first=False, last=False):
                for s in range(SPP):
                    n = SPP * p + s
                    start, end = first and s == 0, last and s == SPP - 1
                    if start:
                        dve.wait_ge(ld_x[1], 16)
                        statistics(1, 1)

                    def maximum(i):
                        dve.wait_ge(s_mm, QT * n + i + 1)
                        dve.tensor_reduce(neg_max[:, i:i + 1], score_ps[i % 2][:, :], AX.X, ALU.max,
                                          negate=True).then_inc(max_ok, 1)

                    def inverse(i):
                        dve.wait_ge(exp_ok, QT * n + i + 1)
                        dve.reciprocal(inv_sum[:, i:i + 1], row_sum[:, i:i + 1]).then_inc(inv_ok, 1)

                    def prob_low(i):
                        dve.wait_ge(p_hi_ok, QT * n + i + 1)
                        dve.tensor_tensor(pT_lo[:, s % 2, :, i * P:(i + 1) * P],
                                          tr_ps[i % 2][:, :].rearrange("p (k q) -> p k q", k=QT),
                                          pT_hi[:, s % 2, :, i * P:(i + 1) * P].bitcast(f32), ALU.subtract).then_inc(p_ok, 1)

                    maximum(0)
                    if not (first and s < 2):
                        y_add(DC * (n - 1), batch_of(s - 2), 1, first and s % 2 == 0)
                    maximum(1)
                    inverse(0)
                    maximum(2)
                    inverse(1)
                    maximum(3)
                    inverse(2)
                    inverse(3)
                    if start:
                        normalise(1, 1, 1)
                        input_lo(1)
                    if first and s in INPUT_AT:
                        b = INPUT_AT[s]
                        dve.wait_ge(ld_x[b], 16)
                        statistics(b, b % 2)
                    if not start:
                        o_low(n, head_slice(p, s - 1))
                    prob_low(0)
                    if not end:
                        q_low(n + 2, head_slice(p, s + 1))
                    prob_low(1)
                    if not end:
                        k_low(n + 2, head_slice(p, s + 1))
                    prob_low(2)
                    prob_low(3)
                    if not start:
                        y_add(DC * (n - 1) + 1, batch_of(s - 1), 0, first and s % 2 == 1)
                    if first and s in INPUT_AT:
                        b = INPUT_AT[s]
                        normalise(b, b, b % 2)

            pair(0, first=True)
            dve.wait_ge(y_zero, 1)
            with dve.Fori(1, PAIRS - 1) as p:
                pair(p)
            pair(PAIRS - 1, last=True)
            N = SPP * PAIRS
            y_add(DC * (N - 1), B - 1, 1, False)
            dve.tensor_copy(pick, ident[0:B, 0:B].unsqueeze(2).to_broadcast([B, B, P])).then_inc(pick_ok, 1)
            dve.wait_ge(mod2_ev, 2)
            magnitude_guard(mod_row[:, 0:D], mod_row[:, 0:D], [guard_t[:, i] for i in range(2)], ga_ok)
            dve.wait_ge(ga_ok, 1)
            at = (GB - GA) * P
            magnitude_guard(mod_row[:, at:at + D], mod_row[:, at:at + D], [guard_t[:, i] for i in range(2)], gb_ok)

            def gated(b):
                for c in range(DC):
                    dve.tensor_scalar(yT[:, c, tokens(b)], yT[:, c, tokens(b)], bo_sb[:, c:c + 1],
                                      modT[:, GA + c, b:b + 1], ALU.add, ALU.mult).then_inc(yg_ok, 1)

            o_low(N, slice(FEAT // P - 1, FEAT // P))
            dve.wait_ge(mod_ok, 3)
            dve.wait_ge(y_ok, DC * (N - 2))
            for b in range(B - 1):
                gated(b)
            for c in range(DC):
                y_add(DC * (N - 1) + c + 1, B - 1, c, False)
            dve.wait_ge(y_ok, DC * N)
            gated(B - 1)

            def ffn_input(b):
                for u in range(2):
                    dve.wait_ge(x1_tr, 2 * b + u + 1)
                    t = b * QT + 2 * u
                    dve.tensor_tensor(x_nat[:, t:t + 2], score_ps[1][:, :].rearrange("p (t d) -> p t d", t=2),
                                      x_nat[:, t:t + 2], ALU.add).then_inc(x1_ok, 1)
                dve.wait_ge(x1_ok, 2 * (b + 1))
                if b >= 2:
                    dve.wait_ge(z2_tr, DC * (b - 1))
                statistics(b, b % 2)
                normalise(B + b, b, b % 2)

            chained = [0]

            def chain(ins):
                chained[0] += 1
                ins.then_inc(router_step, 1)
                dve.wait_ge(router_step, chained[0])

            def wide(v):
                return v.unsqueeze(2).to_broadcast([P, QT, EXP])

            def first_greatest(src, most, hot):
                chain(dve.tensor_reduce(most, src[:, :, :], AX.X, ALU.max))
                chain(dve.tensor_tensor(cand[:, :, :], src[:, :, :], wide(most), ALU.is_equal))
                chain(dve.scalar_tensor_tensor(out=cand[:, :, :], in0=cand[:, :, :], scalar=-float(EXP), in1=iota8[:, :, :],
                                               op0=ALU.mult, op1=ALU.add))
                chain(dve.tensor_reduce(top[:, 7], cand[:, :, :], AX.X, ALU.min))
                chain(dve.tensor_tensor(hot[:, :, :], cand[:, :, :], wide(top[:, 7]), ALU.is_equal))

            def router(b):
                dve.wait_ge(ag_mm, b + 1)
                for u in range(2):
                    chain(dve.tensor_copy(logit[:, 2 * u:2 * u + 2], ag_view(u)[:, :, ER:ER + EXP]))
                first_greatest(logit, top[:, 0], hot1)
                chain(dve.scalar_tensor_tensor(out=masked[:, :, :], in0=hot1[:, :, :], scalar=-3.0e38, in1=logit[:, :, :],
                                               op0=ALU.mult, op1=ALU.add))
                first_greatest(masked, top[:, 1], hot2)
                dve.tensor_tensor(top[:, 3], top[:, 1], top[:, 0], ALU.subtract).then_inc(margin_ok, 1)
                dve.wait_ge(e2_ok, b + 1)
                chain(dve.tensor_scalar(top[:, 5], top[:, 4], 1.0, None, ALU.add))
                chain(dve.reciprocal(top[:, 6], top[:, 5]))
                chain(dve.tensor_scalar(top[:, 5], top[:, 6], LORA_ALPHA, None, ALU.mult))
                chain(dve.tensor_tensor(top[:, 6], top[:, 5], top[:, 4], ALU.mult))
                chain(dve.tensor_tensor(hot1[:, :, :], hot1[:, :, :], wide(top[:, 5]), ALU.mult))
                chain(dve.tensor_tensor(hot2[:, :, :], hot2[:, :, :], wide(top[:, 6]), ALU.mult))
                chain(dve.tensor_tensor(wmat[:, :, :], hot1[:, :, :], hot2[:, :, :], ALU.add))
                if b:
                    dve.wait_ge(hw_tr, b)
                for u in range(2):
                    dve.tensor_tensor(hw[:, 2 * u:2 * u + 2].rearrange("p t (e r) -> p t e r", e=EXP),
                                      ag_view(u)[:, :, 0:ER].rearrange("p t (e r) -> p t e r", e=EXP),
                                      wmat[:, 2 * u:2 * u + 2].unsqueeze(3).to_broadcast([P, 2, EXP, RANK]),
                                      ALU.mult).then_inc(hw_ok, 1)

            def result(b):
                for u in range(2):
                    i = 2 * b + u
                    dve.wait_ge(f_mm, i + 1)
                    if b:
                        dve.wait_ge(stored[u], 16 * b)
                    dve.tensor_tensor(res[:, u], (o_ps, y_ps)[u][:, :].rearrange("p (t d) -> p t d", t=2),
                                      gb_row[:, b:b + 1].to_broadcast([P, 2, D]), ALU.mult).then_inc(res_t, 1)
                    dve.wait_ge(res_t, i + 1)
                    dve.tensor_tensor(res[:, u], res[:, u], x_nat[:, 2 * i:2 * i + 2], ALU.add).then_inc(res_ok, 1)

            dve.wait_ge(gbb_ok, 2)
            dve.wait_ge(iota_ok, EXP)
            ffn_input(0)
            for b in range(B):
                router(b)
                if b + 1 < B:
                    ffn_input(b + 1)
                result(b)

        @block.tensor
        def _(pe):
            def three(dst, a, b_, first, last, group_check=True):
                (a_hi, a_lo), (b_hi, b_lo) = a, b_
                pe.matmul(dst, a_hi, b_hi, start=first, stop=False)
                pe.matmul(dst, a_hi, b_lo, start=False, stop=False)
                return pe.matmul(dst, a_lo, b_hi, start=False, stop=last)

            pe.wait_ge(ident_ok, 1)
            pe.wait_ge(ld_c, 16)
            pe.transpose(o_ps[:, 0:B * DC], c_raw[:, :], ident[0:B * DC, 0:B * DC]).then_inc(c_tr, 1)
            pe.wait_ge(ld_wmod, 16)
            pe.wait_ge(silu_ok, 1)
            silu = c_silu[:, :].rearrange("p (b c) -> p c b", c=DC)
            for j in range(SA, GA):
                for c in range(DC):
                    ins = pe.matmul(ky_ps[:, j * B:(j + 1) * B], wmod_1[:, c, j * P:(j + 1) * P], silu[:, c],
                                    start=(c == 0), stop=(c == DC - 1))
            ins.then_inc(mod_mm, 1)

            def transpose_input(b, banks):
                pe.wait_ge(z_ok, QT * (b + 1))
                for c in range(DC):
                    for t in range(QT):
                        ins = pe.transpose(banks[c][:, t * P:(t + 1) * P], z[:, b % 2, t, c * P:(c + 1) * P], ident[:, :])
                    ins.then_inc(h_tr, 1)

            transpose_input(0, tr_ps)
            pe.wait_ge(ld_vec, 16 * 4)
            pe.transpose(y_ps[:, 0:VECS], vec_raw[:, :], ident[0:VECS, 0:VECS]).then_inc(vec_tr, 1)

            def project(dst, m, j, b):
                for c in range(DC):
                    cut = (slice(None), c, slice(j * HD, (j + 1) * HD))
                    ins = three(dst[:, :], (w_hi[m][cut], w_lo[m][cut]),
                                (hT_hi[:, c, tokens(b)], hT_lo[:, c, tokens(b)]), c == 0, c == DC - 1)
                return ins

            def project_v(b, half):
                for t in range(2):
                    first = b * S + (2 * half + t) * P
                    for c in range(DC):
                        cut = (slice(None), c, slice(first, first + P))
                        ins = three(qv_ps[:, t * PW:(t + 1) * PW], (hT_hi[cut], hT_lo[cut]),
                                    (w_hi["v"][:, c], w_lo["v"][:, c]), c == 0, c == DC - 1)
                return ins

            pe.wait_ge(h_lo, DC)
            pe.wait_ge(w_ok["q"], 1)
            project(qv_ps, "q", 0, 0).then_inc(q_mm, 1)
            pe.wait_ge(w_ok["k"], 1)
            pe.wait_ge(mod_ok, 2)
            project(ky_ps, "k", 0, 0).then_inc(k_mm, 1)
            pe.wait_ge(w_ok["v"], 1)
            pe.wait_ge(q_ok, 1)
            project_v(0, 0).then_inc(v_mm, 1)
            pe.wait_ge(v32_ok, 1)
            project_v(0, 1).then_inc(v_mm, 1)

            def weighted(par_step, vpar, j, kt):
                cut = (slice(None), vpar, kt, slice(j * HD, (j + 1) * HD))
                return three(o_ps[:, :], (v_hi[cut], v_lo[cut]), (pT_hi[:, par_step, kt], pT_lo[:, par_step, kt]),
                             kt == 0, kt == QT - 1)

            def out_project(c, j):
                cut = (slice(None), j, slice(c * P, (c + 1) * P))
                return three((y_ps, ky_ps)[c][:, :], (w_hi["o"][cut], w_lo["o"][cut]), (o_hi[:, :], o_lo[:, :]), True, True)

            def pair(p, first=False, last=False):
                for s in range(SPP):
                    n = SPP * p + s
                    b = batch_of(s)
                    prev = (s - 1) % SPP
                    nxt = (s + 1) % SPP
                    start, end = first and s == 0, last and s == SPP - 1
                    early = first and s < 2
                    pe.wait_ge(q_ok, n + 1)
                    pe.wait_ge(k_ok, n + 1)
                    for i in range(QT):
                        if not (start and i < 2):
                            pe.wait_ge(exp_ok, QT * n + i - 1)
                        cut = (slice(None), slice(i * P, (i + 1) * P))
                        three(score_ps[i % 2][:, :], (q_hi[cut], q_lo[cut]), (k_hi[:, :], k_lo[:, :]),
                              True, True).then_inc(s_mm, 1)
                        if not start:
                            if i == 0:
                                pe.wait_ge(p_ok, QT * n)
                                if first and s == 1:
                                    pe.wait_ge(h_hi, DC * 2)
                                pe.wait_ge(v_ok, n + s % 2)
                                if not early:
                                    pe.wait_ge(o_ok, n - 1)
                            ins = weighted((s - 1) % 2, batch_of(prev) % 2, prev % 2, i)
                            if i == QT - 1:
                                ins.then_inc(o_mm, 1)
                    if start:
                        pe.wait_ge(vec_ok, 2)
                        transpose_input(1, (o_ps, y_ps))

                    def transpose_probs(i):
                        pe.wait_ge(prob_ok, QT * n + i + 1)
                        if first and s - 1 in INPUT_AT and i < DC:
                            pe.wait_ge(h_hi, DC * INPUT_AT[s - 1] + i + 1)
                        if not (start and i < 2):
                            pe.wait_ge(p_ok, QT * n + i - 1)
                        for kt in range(QT):
                            ins = pe.transpose(tr_ps[i % 2][:, kt * P:(kt + 1) * P], prob[:, i, kt * P:(kt + 1) * P], ident[:, :])
                        ins.then_inc(p_tr, 1)

                    transpose_probs(0)
                    if not end:
                        if first:
                            pe.wait_ge(h_lo, DC * (batch_of(nxt) + 1 if nxt else B))
                        if s >= SPP - 1 or s == 0:
                            pe.wait_ge(w_ok["q"], 2 * p + (3 if s else 2))
                        pe.wait_ge(v32_ok, n + 2)
                        project(qv_ps, "q", nxt % 2, batch_of(nxt)).then_inc(q_mm, 1)
                    if end:
                        pe.wait_ge(ld_wmod2, 16)
                        pe.wait_ge(v32_ok, n + 1)
                        pe.wait_ge(y_ok, DC * (n - 1))
                        for i in range(2):
                            for c in range(DC):
                                ins = pe.matmul((qv_ps, ky_ps)[i][0:B, :], silu[:, c], wmod_2[:, c, i * S:(i + 1) * S],
                                                start=(c == 0), stop=(c == DC - 1))
                            ins.then_inc(mod2_mm, 1)
                    transpose_probs(1)
                    if not end:
                        if s >= SPP - 1 or s == 0:
                            pe.wait_ge(w_ok["k"], 2 * p + (3 if s else 2))
                        if not early:
                            pe.wait_ge(y_ok, DC * (n - 1))
                        project(ky_ps, "k", nxt % 2, batch_of(nxt)).then_inc(k_mm, 1)
                    transpose_probs(2)
                    if not (last and s >= SPP - SPB):
                        if first:
                            pe.wait_ge(h_lo, DC * min(b + 2, B))
                        if s == SPP - SPB:
                            pe.wait_ge(w_ok["v"], p + 2)
                        pe.wait_ge(q_ok, n + 2)
                        project_v((b + 1) % B, s % 2).then_inc(v_mm, 1)
                    transpose_probs(3)
                    if not start:
                        pe.wait_ge(o_ok, n)
                        if s == 1 or s == 2:
                            pe.wait_ge(w_ok["o"], 2 * p + s)
                        if not early:
                            pe.wait_ge(y_ok, DC * (n - 1) - 1)
                        out_project(0, prev % 2).then_inc(y_mm, 1)
                        if not end:
                            pe.wait_ge(k_ok, n + 2)
                        else:
                            pe.wait_ge(mod2_ev, 2)
                        out_project(1, prev % 2).then_inc(y_mm, 1)
                    if first and s in INPUT_AT:
                        pe.wait_ge(p_ok, QT * (n + 1))
                        transpose_input(INPUT_AT[s], tr_ps)

            pair(0, first=True)
            with pe.Fori(1, PAIRS - 1) as p:
                pair(p)
            pair(PAIRS - 1, last=True)

            N = SPP * PAIRS
            pe.wait_ge(p_ok, QT * N)
            pe.wait_ge(o_ok, N - 1)
            for kt in range(QT):
                ins = weighted((N - 1) % 2, (B - 1) % 2, 1, kt)
            ins.then_inc(o_mm, 1)
            pe.wait_ge(ga_ok, 1)
            for j in range(GB - GA):
                ins = pe.transpose(qv_ps[:, j * B:(j + 1) * B], mod_row[:, j * P:(j + 1) * P], ident[0:B, 0:B])
            ins.then_inc(mod2_tr, 1)
            pe.wait_ge(gb_ok, 1)
            pe.wait_ge(pick_ok, 1)
            at = (GB - GA) * P
            pe.wait_ge(exp_ok, QT * N)
            for b in range(B):
                ins = pe.matmul(score_ps[b // 2][:, (b % 2) * D:(b % 2 + 1) * D], pick[:, b], mod_row[:, at:at + D],
                                start=True, stop=True)
                if b % 2:
                    ins.then_inc(gbb_mm, 1)
            pe.wait_ge(o_ok, N)
            pe.wait_ge(y_ok, DC * (N - 1))
            for c in range(DC):
                out_project(c, 1).then_inc(y_mm, 1)
            pe.wait_ge(ld_ffn, 16 * (3 + O // P))
            pe.wait_ge(mod_ok, 5)
            for c in range(DC):
                for r in range(O // P):
                    pe.transpose(tr_ps[0][:, c * O + r * P:c * O + (r + 1) * P], w_raw[:, r, c * P:(c + 1) * P], ident[:, :])
                at = c * (ER + EXP)
                pe.transpose(tr_ps[1][:, at:at + ER], a_raw[:, c * P:(c + 1) * P], ident[:, :])
                pe.transpose(tr_ps[1][:, at + ER:at + ER + EXP], g_raw[:, c * P:(c + 1) * P], ident[0:EXP, 0:EXP])
            for r in range(O // P):
                ins = pe.transpose(qv_ps[:, r * P:(r + 1) * P], b_raw[:, r].rearrange("p e r -> p (e r)"), ident[:, :])
            ins.then_inc(ffn_tr, 1)

            def rows_of_y(b):
                for u in range(2):
                    if 2 * b + u >= 1:
                        pe.wait_ge(x1_ok, 2 * b + u)
                    pe.wait_ge(yg_ok, DC * (b + 1))
                    for t in range(2):
                        for c in range(DC):
                            first = b * S + (2 * u + t) * P
                            ins = pe.transpose(score_ps[1][:, t * D + c * P:t * D + (c + 1) * P], yT[:, c, first:first + P], ident[:, :])
                    ins.then_inc(x1_tr, 1)

            pe.wait_ge(gbb_ok, 2)
            rows_of_y(0)
            pe.wait_ge(ffn_ev, 3)
            for b in range(B):
                pe.wait_ge(z_ok, QT * (B + b + 1))
                for c in range(DC):
                    if b:
                        pe.wait_ge(z2_ev, DC * (b - 1) + c + 1)
                    for t in range(QT):
                        ins = pe.transpose(tr_ps[c][:, t * P:(t + 1) * P], z[:, b % 2, t, c * P:(c + 1) * P], ident[:, :])
                    ins.then_inc(z2_tr, 1)
                pe.wait_ge(z2_ev, DC * (b + 1))
                if b:
                    pe.wait_ge(hw_ok, 2 * b)
                for t in range(QT):
                    for c in range(DC):
                        ins = pe.matmul(ag_view(t // 2)[:, t % 2], h2T[:, b % 2, c, t * P:(t + 1) * P], agT[:, c],
                                        start=(c == 0), stop=(c == DC - 1))
                ins.then_inc(ag_mm, 1)
                if b + 1 < B:
                    rows_of_y(b + 1)
                pe.wait_ge(hw_ok, 2 * (b + 1))
                if b:
                    pe.wait_ge(hwT_ok, b)
                for t in range(QT):
                    ins = pe.transpose(score_ps[0][:, t * P:(t + 1) * P], hw[:, t], ident[:, :])
                ins.then_inc(hw_tr, 1)
                pe.wait_ge(hwT_ok, b + 1)
                for u in range(2):
                    if b:
                        pe.wait_ge(res_t, 2 * (b - 1) + u + 1)
                    for t in range(2):
                        k = 2 * u + t
                        dst = (o_ps, y_ps)[u][:, t * D:(t + 1) * D]
                        for c in range(DC):
                            pe.matmul(dst, h2T[:, b % 2, c, k * P:(k + 1) * P], wT[:, c], start=(c == 0), stop=False)
                        ins = pe.matmul(dst, hwT[:, k * P:(k + 1) * P], bT[:, :], start=False, stop=True)
                    ins.then_inc(f_mm, 1)


_INS = ["L0_attn_x", "L0_attn_wq_codes", "L0_attn_wq_scales", "L0_attn_bq", "L0_attn_wk_codes", "L0_attn_wk_scales",
        "L0_attn_bk", "L0_attn_wv_codes", "L0_attn_wv_scales", "L0_attn_bv", "L0_attn_wo_codes", "L0_attn_wo_scales",
        "L0_attn_bo", "L0_ffn_W", "L0_ffn_gate_w", "L0_ffn_A", "L0_ffn_B", "L0_c", "L0_wmod"]
_OUTS = [((4, 512, 256), "float32")]


def kernel(**inputs):
    import numpy as _np
    import concourse.bacc as _bacc
    from concourse import mybir as _mybir
    from concourse.bass_utils import run_bass_kernel_spmd as _run

    nc = _bacc.Bacc("TRN2", target_bir_lowering=False, num_devices=1)
    arrays, args = {}, []
    for name in _INS:
        a = _np.ascontiguousarray(inputs[name])
        arrays[f"in_{name}_dram"] = a
        args.append(nc.dram_tensor(f"in_{name}_dram", a.shape, _mybir.dt.from_np(a.dtype), kind="ExternalInput").ap())
    for i, (shape, dtype) in enumerate(_OUTS):
        dt = _mybir.dt.from_np(_np.dtype(dtype))
        args.append(nc.dram_tensor(f"out_{i}_dram", shape, dt, kind="ExternalOutput").ap())
    bass_adaln_mxfp4_attention_moe_lora_kernel(nc, *args)
    r = _run(nc, [arrays], core_ids=[0])
    got = tuple(r.results[0][f"out_{i}_dram"] for i in range(len(_OUTS)))
    return got[0]
```

```python
import concourse.bass as bass
from concourse import mybir
from contextlib import ExitStack


def bass_adaln_mxfp4_attention_moe_lora_kernel(
    nc: bass.Bass,
    x: bass.AP,
    wq_codes: bass.AP,
    wq_scales: bass.AP,
    bq: bass.AP,
    wk_codes: bass.AP,
    wk_scales: bass.AP,
    bk: bass.AP,
    wv_codes: bass.AP,
    wv_scales: bass.AP,
    bv: bass.AP,
    wo_codes: bass.AP,
    wo_scales: bass.AP,
    bo: bass.AP,
    ffn_w: bass.AP,
    gate_w: bass.AP,
    lora_a: bass.AP,
    lora_b: bass.AP,
    cond: bass.AP,
    wmod: bass.AP,
    out: bass.AP,
):
    f32 = mybir.dt.float32
    f32r = mybir.dt.float32r
    ALU = mybir.AluOpType
    ACT = mybir.ActivationFunctionType
    AX = mybir.AxisListType

    B, S, D = x.shape
    FEAT = wq_codes.shape[1]
    HD = 128
    P = 128
    PAIRS = FEAT // (2 * HD)
    PW = 2 * HD
    DC = D // P
    QT = S // P
    BLK = D // wq_scales.shape[0]
    NB = P // BLK
    SPB = 2
    SPP = SPB * B
    EXP, RANK = lora_a.shape[0], lora_a.shape[1]
    ER = EXP * RANK
    O = ffn_w.shape[0]
    LORA_ALPHA = 16.0
    EPS = 1e-5
    MODS = wmod.shape[1] // P
    SA, CA, GA, SB, CB, GB = (DC * i for i in range(6))
    NT = B * QT
    SCORE_SCALE = float(HD) ** -0.5
    assert D == 256 and S == 512 and ER == P and B == 4

    with ExitStack() as ctx:
        def sb(name, shape, dt=f32):
            return ctx.enter_context(nc.sbuf_tensor(name, shape, dt))

        def sem(name):
            return ctx.enter_context(nc.semaphore(name))

        ident = sb("ident", [P, P])
        x_nat = sb("x_nat", [P, NT, D])
        hT_hi = sb("hT_hi", [P, DC, B * S], f32r)
        hT_lo = sb("hT_lo", [P, DC, B * S], f32r)
        hT32 = sb("hT32", [P, 2, S])
        z = sb("z", [P, 2, QT, D])
        yT = sb("yT", [P, DC, B * S])
        wmod_1 = yT[:, :, 0:(GA - SA) * P]
        w_hi = {m: sb(f"w{m}_hi", [P, 2, PW], f32r) for m in "qkvo"}
        w_lo = {m: sb(f"w{m}_lo", [P, 2, PW], f32r) for m in "qkvo"}
        stage = sb("stage", [P, 12, 2 * PW])

        def staged(i):
            return {m: stage[:, i + 3 * "qkvo".index(m)].rearrange("p (c n) -> p c n", c=2) for m in "qkvo"}

        codes, scales, w32 = staged(0), staged(1), staged(2)
        q_hi, q_lo = sb("q_hi", [P, S], f32r), sb("q_lo", [P, S], f32r)
        k_hi, k_lo = sb("k_hi", [P, S], f32r), sb("k_lo", [P, S], f32r)
        v_hi = sb("v_hi", [P, 2, QT, PW], f32r)
        v_lo = sb("v_lo", [P, 2, QT, PW], f32r)
        v32 = sb("v32", [P, 2, PW])
        prob = sb("prob", [P, QT, S])
        pT_hi = sb("pT_hi", [P, 2, QT, S], f32r)
        pT_lo = sb("pT_lo", [P, 2, QT, S], f32r)
        o_hi, o_lo = sb("o_hi", [P, S], f32r), sb("o_lo", [P, S], f32r)
        neg_max = sb("neg_max", [P, QT])
        row_sum = sb("row_sum", [P, QT])
        inv_sum = sb("inv_sum", [P, QT])
        NH = FEAT // P
        VECS = 3 * NH + DC
        c_raw = sb("c_raw", [B * DC, P])
        vec_raw = sb("vec_raw", [VECS, P])
        vecT = sb("vecT", [P, VECS])
        bias = vecT[:, 0:3 * NH].rearrange("p (n h) -> p n h", n=3)
        bo_sb = vecT[:, 3 * NH:VECS]
        bias_now = sb("bias_now", [P, 3, 2])
        c_exp = sb("c_exp", [P, B * DC])
        c_silu = sb("c_silu", [P, B * DC])
        modT = sb("modT", [P, MODS, B])
        ga_bo = sb("ga_bo", [P, DC, B])
        gb_row = sb("gb_row", [P, B, D])
        stats = sb("stats", [P, B, QT, 6])
        mv = sb("mv", [P, B, QT, 2])
        rstd = sb("rstd", [P, B, QT])
        var_eps = sb("var_eps", [P, B, QT])
        minus_half = sb("minus_half", [P, 1])
        wmod_2 = stage[:, 0:4].rearrange("p i n -> p (i n)").rearrange("p (c n) -> p c n", c=DC)
        w_raw = stage[:, 4].rearrange("p (c d) -> p c d", c=O // P)
        a_raw = stage[:, 5, 0:D]
        g_raw = stage[0:EXP, 5, D:2 * D]
        b_raw = stage[:, 6, 0:O].rearrange("p (c e r) -> p c e r", c=O // P, e=EXP)
        mod_row = stage[0:B, 7:9].rearrange("b i n -> b (i n)")
        guard_t = stage[0:B, 9].rearrange("b (i n) -> b i n", i=2)
        pick = stage[0:B, 10].rearrange("k (b n) -> k b n", b=B)
        lora = stage[:, 0:4].rearrange("p i (t n) -> p (i t) n", n=ER)
        hwT = [stage[:, i] for i in (4, 5, 6, 9)]
        wT = sb("wT", [P, DC, O])
        agT = sb("agT", [P, DC, ER + EXP])
        bT = sb("bT", [P, O])
        w_gb = [v.rearrange("p (c o) -> p c o", c=DC) for v in (hT32[:, 0], hT32[:, 1], stage[:, 10], stage[:, 11])]
        b_gb = [v32[:, 0], v32[:, 1], stage[:, 7, 0:O], stage[:, 7, O:2 * O]]
        h2T_a = sb("h2T", [P, 2, DC, S])
        h2T_b = prob[:, :, :].rearrange("p (b c) s -> p b c s", c=DC)
        h2T = [h2T_a[:, 0], h2T_a[:, 1], h2T_b[:, 0], h2T_b[:, 1]]
        GROUPS = 2
        GT = NT // GROUPS
        iota8 = sb("iota8", [P, GT, EXP])
        logit = sb("logit", [P, NT, EXP])
        masked = sb("masked", [P, GT, EXP])
        cand = sb("cand", [P, GT, EXP])
        hot1 = sb("hot1", [P, GT, EXP])
        hot2 = sb("hot2", [P, GT, EXP])
        top = sb("top", [P, 8, GT])
        wmat = sb("wmat", [P, NT, EXP])

        def bank(name):
            return ctx.enter_context(nc.psum_tensor(name, [P, S], f32))

        score_ps = [bank("score0"), bank("score1")]
        tr_ps = [bank("tr0"), bank("tr1")]
        qv_ps, ky_ps, o_ps, y_ps = bank("qv"), bank("ky"), bank("o"), bank("y")

        f_banks = [o_ps, y_ps, score_ps[0], score_ps[1], qv_ps, ky_ps, tr_ps[0], tr_ps[1]]

        ident_0, ident_ok, iota_ok, half_ok = (sem(n) for n in ("ident_0", "ident_ok", "iota_ok", "half_ok"))
        ld_c, c_tr, ld_vec, vec_tr, vec_ok, ld_wmod, ld_wmod2, ld_ffn = (
            sem(n) for n in ("ld_c", "c_tr", "ld_vec", "vec_tr", "vec_ok", "ld_wmod", "ld_wmod2", "ld_ffn"))
        ld_x_first = sem("ld_x_first")
        ld_x = [sem(f"ld_x{b}") for b in range(B)]
        ld_w = {m: sem(f"ld_w{m}") for m in "qkvo"}
        c_exped, silu_step, mod_mm, mod_ok = (sem(n) for n in ("c_exped", "silu_step", "mod_mm", "mod_ok"))
        mod2_mm, mod2_ev, pick_ok, ga_ok, gb_ok, mod2_tr, gbb_mm, gbb_ok = (
            sem(n) for n in ("mod2_mm", "mod2_ev", "pick_ok", "ga_ok", "gb_ok", "mod2_tr", "gbb_mm", "gbb_ok"))
        silu_ok = sem("silu_ok")
        bias_ok = sem("bias_ok")
        ffn_tr, ffn_ev = sem("ffn_tr"), sem("ffn_ev")
        ln_step, ln_var, ln_rstd, z_ok = (sem(n) for n in ("ln_step", "ln_var", "ln_rstd", "z_ok"))
        h_tr, h_ev, h_hi, h_lo = (sem(n) for n in ("h_tr", "h_ev", "h_hi", "h_lo"))
        w_prod = {m: sem(f"w{m}_prod") for m in "qkvo"}
        wq_scaled = sem("wq_scaled")
        w_hi_ok = {m: sem(f"w{m}_hi_ok") for m in "qkvo"}
        w_ok = {m: sem(f"w{m}_ok") for m in "qkvo"}
        q_mm, q_hi_ok, q_ok = sem("q_mm"), sem("q_hi_ok"), sem("q_ok")
        k_mm, k_hi_ok, k_ok = sem("k_mm"), sem("k_hi_ok"), sem("k_ok")
        v_mm, v_hi_ok, v32_ok, v_ok = sem("v_mm"), sem("v_hi_ok"), sem("v32_ok"), sem("v_ok")
        s_mm, max_ok, exp_ok, inv_ok, prob_ok = (sem(n) for n in ("s_mm", "max_ok", "exp_ok", "inv_ok", "prob_ok"))
        p_tr, p_hi_ok, p_ok = sem("p_tr"), sem("p_hi_ok"), sem("p_ok")
        o_mm, o_hi_ok, o_ok = sem("o_mm"), sem("o_hi_ok"), sem("o_ok")
        y_zero, y_mm, y_ok = sem("y_zero"), sem("y_mm"), sem("y_ok")
        yg_ok = [sem(f"yg_ok{b}") for b in range(B)]
        x1_tr, x1_ok, z2_tr, z2_ev = (sem(n) for n in ("x1_tr", "x1_ok", "z2_tr", "z2_ev"))
        ag_mm, router_step, margin_ok, e2_ok, f_mm = (sem(n) for n in ("ag_mm", "router_step", "margin_ok", "e2_ok", "f_mm"))
        ag_ev, wmat_ok, wg_ok = sem("ag_ev"), sem("wmat_ok"), [sem(f"wg_ok{b}") for b in range(B)]
        ga_bo_ok = sem("ga_bo_ok")
        hw_ok, hw_tr, hwT_ok, res_ok, stored = (sem(n) for n in ("hw_ok", "hw_tr", "hwT_ok", "res_ok", "stored"))

        CODES = dict(q=wq_codes, k=wk_codes, v=wv_codes, o=wo_codes)
        SCALES = dict(q=wq_scales, k=wk_scales, v=wv_scales, o=wo_scales)
        LDW = 16 * 3

        INPUT_AT = {1: 2, 3: 3}

        def batch_of(s):
            return (s % SPP) // SPB

        def tokens(b):
            return slice(b * S, (b + 1) * S)

        def ag_view(u):
            return (qv_ps, ky_ps)[u][:, 0:2 * (ER + EXP)].rearrange("p (t n) -> p t n", t=2)

        def hwT_bank(b):
            return (tr_ps[0], tr_ps[1], o_ps, y_ps)[b]

        block = ctx.enter_context(nc.Block())

        @block.sync
        def _(sp):
            sp.dma_start(c_raw[:, :], cond.rearrange("b (c p) -> (b c) p", p=P)).then_inc(ld_c, 16)
            first = x[0].rearrange("(t p) d -> p t d", p=P)
            sp.dma_start(x_nat[:, 0:2], first[:, 0:2]).then_inc(ld_x_first, 16)
            sp.dma_start(x_nat[:, 2:QT], first[:, 2:QT]).then_inc(ld_x[0], 16)
            cols = wmod.rearrange("(c p) n -> p c n", p=P)
            sp.dma_start(wmod_1, cols[:, :, 0:GA * P]).then_inc(ld_wmod, 16)

            def load_weights(m, p):
                if m == "o":
                    rows = CODES[m].rearrange("(h p) d -> p h d", p=P)
                    sp.dma_start(codes[m][:, :, :], rows[:, bass.ds(2 * p, 2), :]).then_inc(ld_w[m], 16)
                    for j in range(2):
                        start = 2 * NB * D * p + j * NB * D
                        src = bass.AP(SCALES[m].tensor, start, [[D, NB], [0, BLK], [1, D]])
                        sp.dma_start(scales[m][:, j], src).then_inc(ld_w[m], 16)
                    return
                cols = CODES[m].rearrange("(c p) f -> p c f", p=P)
                sp.dma_start(codes[m][:, :, :], cols[:, :, bass.ds(PW * p, PW)]).then_inc(ld_w[m], 16)
                for c in range(DC):
                    start = PW * p + c * NB * FEAT
                    src = bass.AP(SCALES[m].tensor, start, [[FEAT, NB], [0, BLK], [1, PW]])
                    sp.dma_start(scales[m][:, c], src).then_inc(ld_w[m], 16)

            for m in "qkv":
                load_weights(m, 0)
            for i, vec in enumerate((bq, bk, bv, bo)):
                sp.dma_start(vec_raw[i * NH:min((i + 1) * NH, VECS), :], vec.rearrange("(h p) -> h p", p=P)).then_inc(ld_vec, 16)
            for b in range(1, B):
                sp.dma_start(x_nat[:, b * QT:(b + 1) * QT], x[b].rearrange("(t p) d -> p t d", p=P)).then_inc(ld_x[b], 16)
            load_weights("o", 0)

            def next_pair(p):
                for m in "vqk":
                    sp.wait_ge(w_ok[m], (1 if m == "v" else 2) * p)
                    load_weights(m, p)
                sp.wait_ge(w_ok["o"], 2 * p)
                load_weights("o", p)

            next_pair(1)
            with sp.Fori(2, PAIRS) as p:
                next_pair(p)

            for m in "vqk":
                sp.wait_ge(w_ok[m], (1 if m == "v" else 2) * PAIRS)
            sp.dma_start(wmod_2, cols[:, :, GA * P:MODS * P]).then_inc(ld_wmod2, 16)
            sp.dma_start(w_raw, ffn_w.rearrange("(c p) d -> p c d", p=P)).then_inc(ld_ffn, 16)
            sp.dma_start(a_raw, lora_a.rearrange("e r d -> (e r) d")).then_inc(ld_ffn, 16)
            sp.dma_start(g_raw, gate_w).then_inc(ld_ffn, 16)
            for c in range(O // P):
                sp.dma_start(b_raw[:, c], lora_b[:, c * P:(c + 1) * P, :].rearrange("e p r -> p e r")).then_inc(ld_ffn, 16)

            for i in range(2 * B):
                sp.wait_ge(res_ok, i + 1)
                rows = out[i // 2, (i % 2) * 2 * P:(i % 2 + 1) * 2 * P, :].rearrange("(t p) d -> p t d", p=P)
                sp.dma_start(rows, x_nat[:, 2 * i:2 * i + 2]).then_inc(stored, 16)
            sp.wait_ge(stored, 16 * 2 * B)

        @block.gpsimd
        def _(pool):
            pool.memset(ident[:, :], 0.0).then_inc(ident_0, 1)
            pool.wait_ge(ident_0, 1)
            pool.affine_select(out=ident[:, :], in_=ident[:, :], compare_op=ALU.not_equal, fill=1.0,
                               base=0, pattern=[[-1, P]], channel_multiplier=1).then_inc(ident_ok, 1)
            pool.memset(minus_half[:, :], -0.5).then_inc(half_ok, 1)
            for e in range(EXP):
                pool.memset(iota8[:, :, e:e + 1], float(e)).then_inc(iota_ok, 1)
            pool.memset(yT[:, DC - 1, tokens(B - 1)], 0.0).then_inc(y_zero, 1)
            pool.wait_ge(half_ok, 1)

            def inverse_std(i):
                pool.wait_ge(ln_var, i + 1)
                pool.tensor_tensor(rstd[:, i % B], var_eps[:, i % B], minus_half[:, :].to_broadcast([P, QT]),
                                   ALU.pow).then_inc(ln_rstd, 1)

            def product(m, p):
                pool.wait_ge(ld_w[m], LDW * (p + 1))
                if m == "q":
                    pool.wait_ge(wq_scaled, p + 1)
                if not (isinstance(p, int) and p == 0):
                    pool.wait_ge(w_ok[m], (1 if m == "v" else 2) * p)
                pool.tensor_tensor(w32[m][:, :, :], codes[m][:, :, :], scales[m][:, :, :], ALU.mult).then_inc(w_prod[m], 1)

            def parts(m, p, j):
                if m == "v":
                    cut, done = (slice(None), slice(None), slice(None)), p
                elif m == "o":
                    cut, done = (slice(None), j, slice(None)), 2 * p + j
                else:
                    cut, done = (slice(None), slice(None), slice(j * HD, (j + 1) * HD)), 2 * p + j
                pool.wait_ge(w_prod[m], p + 1)
                pool.tensor_tensor(w_hi[m][cut], codes[m][cut], scales[m][cut], ALU.mult).then_inc(w_hi_ok[m], 1)
                pool.wait_ge(w_hi_ok[m], done + 1)
                pool.tensor_tensor(w_lo[m][cut], w32[m][cut], w_hi[m][cut].bitcast(f32), ALU.subtract).then_inc(w_ok[m], 1)

            inverse_std(0)
            for m in "qv":
                product(m, 0)
                for j in range(1 if m == "v" else 2):
                    parts(m, 0, j)

            def v_low(count, par, half):
                pool.wait_ge(v_hi_ok, count)
                pool.wait_ge(v32_ok, count)
                pool.tensor_tensor(v_lo[:, par, 2 * half:2 * half + 2, :], v32[:, :, :],
                                   v_hi[:, par, 2 * half:2 * half + 2, :].bitcast(f32), ALU.subtract).then_inc(v_ok, 1)

            v_low(1, 0, 0)
            inverse_std(1)
            v_low(2, 0, 1)

            def pair(p, first=False, last=False):
                for s in range(SPP):
                    n = SPP * p + s
                    for i in range(QT):
                        pool.wait_ge(inv_ok, QT * n + i + 1)
                        pool.tensor_tensor(prob[:, i], prob[:, i], inv_sum[:, i:i + 1].to_broadcast([P, S]),
                                           ALU.mult).then_inc(prob_ok, 1)
                    if first and s in INPUT_AT:
                        inverse_std(INPUT_AT[s])
                    if first and s == 0:
                        product("o", 0)
                    if s < 2:
                        if not first:
                            pool.wait_ge(y_mm, DC * (n - 1))
                        parts("o", p, s)
                    elif not last:
                        if s < 6:
                            product("vqko"[s - 2], p + 1)
                        else:
                            pool.wait_ge(k_mm, n + 1)
                            parts("q", p + 1, s - 6)
                            parts("k", p + 1, s - 6)
                    if not (last and s >= SPP - SPB):
                        v_low(n + 3, (batch_of(s) + 1) % 2, s % 2)
                    if s == 5 and not last:
                        parts("v", p + 1, 0)

            pair(0, first=True)
            with pool.Fori(1, PAIRS - 1) as p:
                pair(p)
            pair(PAIRS - 1, last=True)
            pool.wait_ge(mod_ok, 3)
            for b in (1, 2):
                pool.wait_ge(y_ok, DC * (SPP * PAIRS - 2))
                for c in range(DC):
                    pool.tensor_scalar(yT[:, c, tokens(b)], yT[:, c, tokens(b)], bo_sb[:, c:c + 1],
                                       modT[:, GA + c, b:b + 1], ALU.add, ALU.mult).then_inc(yg_ok[b], 1)

            def times_gb(b):
                pool.tensor_tensor(w_gb[b], wT[:, :, :], gb_row[:, b:b + 1].to_broadcast([P, DC, O]), ALU.mult).then_inc(wg_ok[b], 1)
                pool.tensor_tensor(b_gb[b], bT[:, :], gb_row[:, b], ALU.mult).then_inc(wg_ok[b], 1)

            for b in range(B):
                inverse_std(B + b)
            pool.wait_ge(ffn_ev, 3)
            pool.wait_ge(gbb_ok, 2)
            for b in range(1, B):
                times_gb(b)
            for b in range(B):
                if b % (B // GROUPS) == 0:
                    pool.wait_ge(wmat_ok, b // (B // GROUPS) + 1)
                rows = lora[:, b * QT:(b + 1) * QT].rearrange("p t (e r) -> p (t e) r", e=EXP)
                weights = wmat[:, b * QT:(b + 1) * QT].rearrange("p t e -> p (t e)")
                pool.tensor_tensor(rows, rows, weights.unsqueeze(2).to_broadcast([P, QT * EXP, RANK]), ALU.mult).then_inc(hw_ok, 1)

        @block.scalar
        def _(act):
            act.wait_ge(c_tr, 1)
            act.activation(c_exp[:, :], o_ps[:, 0:B * DC], ACT.Exp, scale=-1.0).then_inc(c_exped, 1)

            def scale_codes(p):
                act.wait_ge(ld_w["q"], LDW * (p + 1))
                act.activation(codes["q"][:, :, :], codes["q"][:, :, :], ACT.Copy, scale=SCORE_SCALE).then_inc(wq_scaled, 1)

            scale_codes(0)
            act.wait_ge(mod_mm, 1)
            act.activation(modT[:, SA:SA + DC], ky_ps[:, 0:DC * B].rearrange("p (j b) -> p j b", b=B), ACT.Copy).then_inc(mod_ok, 1)
            act.activation(modT[:, CA:CA + DC], ky_ps[:, DC * B:2 * DC * B].rearrange("p (j b) -> p j b", b=B), ACT.Copy,
                           bias=1.0).then_inc(mod_ok, 1)
            act.wait_ge(mod_ok, 2)

            def input_high(b, c, banks):
                act.wait_ge(h_tr, DC * b + c + 1)
                if b:
                    act.wait_ge(h_lo, DC * (b - 1) + c + 1)
                for dst, done in ((hT32[:, c], h_ev), (hT_hi[:, c, tokens(b)], h_hi)):
                    act.activation(dst, banks[c][:, :], ACT.Identity, bias=modT[:, SA + c, b:b + 1],
                                   scale=modT[:, CA + c, b:b + 1]).then_inc(done, 1)

            for c in range(DC):
                input_high(0, c, tr_ps)
            act.wait_ge(vec_ok, 2)
            act.activation(bias_now[:, 0:2], bias[:, 0:2, 0:2], ACT.Copy).then_inc(bias_ok, 1)
            act.wait_ge(bias_ok, 1)

            def q_high(count, j):
                act.wait_ge(q_mm, count)
                act.activation(q_hi[:, :], qv_ps[:, :], ACT.Identity, bias=bias_now[:, 0, j:j + 1]).then_inc(q_hi_ok, 1)

            def k_high(count, j):
                act.wait_ge(k_mm, count)
                act.activation(k_hi[:, :], ky_ps[:, :], ACT.Identity, bias=bias_now[:, 1, j:j + 1]).then_inc(k_hi_ok, 1)

            def v_high(count, par, half):
                act.wait_ge(v_mm, count)
                ps = qv_ps[:, :].rearrange("p (t f) -> p t f", t=2)
                act.activation(v_hi[:, par, 2 * half:2 * half + 2, :], ps, ACT.Copy).then_inc(v_hi_ok, 1)
                if count_is_late(count):
                    act.wait_ge(v_ok, count - 1)
                act.activation(v32[:, :, :], ps, ACT.Copy).then_inc(v32_ok, 1)

            def count_is_late(count):
                return not (isinstance(count, int) and count == 1)

            def mod_columns(ps, i):
                return ps[:, i * DC * B:(i + 1) * DC * B].rearrange("p (j b) -> p j b", b=B)

            def gb_rows(i):
                act.wait_ge(gbb_mm, i + 1)
                act.activation(gb_row[:, 2 * i:2 * i + 2], (o_ps, y_ps)[i][:, :].rearrange("p (b d) -> p b d", b=2),
                               ACT.Copy).then_inc(gbb_ok, 1)

            def gated(b):
                act.wait_ge(y_ok, DC * (SPP * PAIRS - (2 if b < B - 1 else 0)))
                for c in range(DC):
                    act.activation(yT[:, c, tokens(b)], yT[:, c, tokens(b)], ACT.Identity, bias=ga_bo[:, c, b:b + 1],
                                   scale=modT[:, GA + c, b:b + 1]).then_inc(yg_ok[b], 1)

            q_high(1, 0)
            k_high(1, 0)
            v_high(1, 0, 0)
            v_high(2, 0, 1)

            def pair(p, first=False, last=False):
                for s in range(SPP):
                    n = SPP * p + s
                    start, end = first and s == 0, last and s == SPP - 1
                    for i in range(QT):
                        act.wait_ge(max_ok, QT * n + i + 1)
                        if not start:
                            act.wait_ge(p_tr, QT * (n - 1) + i + 1)
                        act.activation(prob[:, i], score_ps[i % 2][:, :], ACT.Exp, bias=neg_max[:, i:i + 1],
                                       accum_out=row_sum[:, i:i + 1]).then_inc(exp_ok, 1)
                        if first and s - 1 in INPUT_AT and i < DC:
                            input_high(INPUT_AT[s - 1], i, tr_ps)
                    if start:
                        for c in range(DC):
                            input_high(1, c, (o_ps, y_ps))
                    if not start:
                        act.wait_ge(o_mm, n)
                        act.activation(o_hi[:, :], o_ps[:, :], ACT.Identity,
                                       bias=bias_now[:, 2, (s - 1) % 2:(s - 1) % 2 + 1]).then_inc(o_hi_ok, 1)

                    def prob_high(i):
                        act.wait_ge(p_tr, QT * n + i + 1)
                        act.activation(pT_hi[:, s % 2, :, i * P:(i + 1) * P],
                                       tr_ps[i % 2][:, :].rearrange("p (k q) -> p k q", k=QT), ACT.Copy).then_inc(p_hi_ok, 1)

                    if s == 0 and not start:
                        act.wait_ge(o_hi_ok, n)
                    prob_high(0)
                    if end:
                        act.wait_ge(mod2_mm, 2)
                        act.activation(mod_row[:, S:2 * S], ky_ps[0:B, :], ACT.Copy).then_inc(mod2_ev, 1)
                    if s == 0:
                        act.activation(bias_now[:, 2], bias[:, 2, bass.ds(2 * p, 2)], ACT.Copy).then_inc(bias_ok, 1)
                        act.wait_ge(bias_ok, 2 * p + 2)
                    if not end:
                        q_high(n + 2, (s + 1) % 2)
                    prob_high(1)
                    if not end:
                        k_high(n + 2, (s + 1) % 2)
                    if end:
                        act.wait_ge(mod2_tr, 1)
                        for i, k in enumerate((GA, SB)):
                            act.activation(modT[:, k:k + DC], mod_columns(qv_ps, i), ACT.Copy).then_inc(mod_ok, 1)
                    prob_high(2)
                    if end:
                        act.wait_ge(mod2_tr, 2)
                        act.activation(modT[:, CB:CB + DC], mod_columns(ky_ps, 0), ACT.Copy, bias=1.0).then_inc(mod_ok, 1)
                    prob_high(3)
                    if end:
                        act.wait_ge(ga_bo_ok, DC)
                        gated(0)
                    if last and s == SPP - 2:
                        act.wait_ge(mod2_mm, 1)
                        act.activation(mod_row[:, 0:S], qv_ps[0:B, :], ACT.Copy).then_inc(mod2_ev, 1)
                    if not (last and s >= SPP - SPB):
                        if s == SPP - 2:
                            act.wait_ge(k_hi_ok, n + 2)
                        v_high(n + 3, (batch_of(s) + 1) % 2, s % 2)
                    if s == SPP - 2 and not last:
                        act.activation(bias_now[:, 0:2], bias[:, 0:2, bass.ds(2 * p + 2, 2)], ACT.Copy).then_inc(bias_ok, 1)
                        act.wait_ge(bias_ok, 2 * p + 3)
                    if s == 2 and not last:
                        scale_codes(p + 1)

            pair(0, first=True)
            with act.Fori(1, PAIRS - 1) as p:
                pair(p)
            pair(PAIRS - 1, last=True)

            act.wait_ge(ffn_tr, 1)
            act.activation(wT[:, :, :], qv_ps[:, :].rearrange("p (c o) -> p c o", c=DC), ACT.Copy).then_inc(ffn_ev, 1)
            act.wait_ge(o_mm, SPP * PAIRS)
            act.activation(o_hi[:, :], o_ps[:, :], ACT.Identity,
                           bias=bias_now[:, 2, 1:2]).then_inc(o_hi_ok, 1)
            act.wait_ge(ffn_tr, 2)
            act.activation(agT[:, :, :], qv_ps[:, 0:DC * (ER + EXP)].rearrange("p (c o) -> p c o", c=DC), ACT.Copy).then_inc(ffn_ev, 1)
            act.activation(bT[:, :], tr_ps[0][:, 0:O], ACT.Copy).then_inc(ffn_ev, 1)
            act.wait_ge(mod_ok, 5)

            def ffn_input_out(b):
                for c in range(DC):
                    act.wait_ge(z2_tr, DC * b + c + 1)
                    act.activation(h2T[b][:, c], tr_ps[c][:, :], ACT.Identity, bias=modT[:, SB + c, b:b + 1],
                                   scale=modT[:, CB + c, b:b + 1]).then_inc(z2_ev, 1)

            def lora_out(b):
                for u in range(2):
                    act.wait_ge(ag_mm, 2 * b + u + 1)
                    t = b * QT + 2 * u
                    act.activation(lora[:, t:t + 2], ag_view(u)[:, :, 0:ER], ACT.Copy).then_inc(ag_ev, 1)
                    act.activation(logit[:, t:t + 2], ag_view(u)[:, :, ER:ER + EXP], ACT.Copy).then_inc(ag_ev, 1)

            def odds(g):
                act.wait_ge(margin_ok, g + 1)
                act.activation(top[:, 4], top[:, 3], ACT.Exp).then_inc(e2_ok, 1)

            def weighted_lora_out(b):
                act.wait_ge(hw_tr, b + 1)
                act.activation(hwT[b], hwT_bank(b)[:, :], ACT.Copy).then_inc(hwT_ok, 1)

            for b in range(B):
                ffn_input_out(b)
                if b == 2:
                    gb_rows(0)
                    gb_rows(1)
                if b == B - 1:
                    odds(0)
                lora_out(b)
                if b == 1:
                    gated(B - 1)
            for b in range(B):
                if b == B // GROUPS:
                    odds(1)
                weighted_lora_out(b)

        @block.vector
        def _(dve):
            dve.wait_ge(c_exped, 1)
            dve.tensor_scalar(c_exp[:, :], c_exp[:, :], 1.0, None, ALU.add).then_inc(silu_step, 1)
            dve.wait_ge(silu_step, 1)
            dve.reciprocal(c_exp[:, :], c_exp[:, :]).then_inc(silu_step, 1)
            dve.wait_ge(silu_step, 2)
            dve.tensor_tensor(c_silu[:, :], c_exp[:, :], o_ps[:, 0:B * DC], ALU.mult).then_inc(silu_ok, 1)

            steps = [0]

            def link(ins):
                steps[0] += 1
                ins.then_inc(ln_step, 1)
                dve.wait_ge(ln_step, steps[0])

            def row_statistics(b, t):
                dve.bn_stats(stats[:, b, t], x_nat[:, b * QT + t]).then_inc(ln_step, 1)
                steps[0] += 1

            def variances(b):
                dve.wait_ge(ln_step, steps[0])
                for t in range(QT):
                    dve.bn_aggr(mv[:, b, t], stats[:, b, t]).then_inc(ln_step, 1)
                steps[0] += QT
                dve.wait_ge(ln_step, steps[0])
                dve.tensor_scalar(var_eps[:, b], mv[:, b, :, 1], EPS, None, ALU.add).then_inc(ln_var, 1)

            def statistics(b):
                for t in range(QT):
                    row_statistics(b, t)
                variances(b)

            def normalise(i):
                b = i % B
                dve.wait_ge(ln_rstd, i + 1)
                for t in range(QT):
                    dve.tensor_scalar(z[:, b % 2, t], x_nat[:, b * QT + t], mv[:, b, t, 0:1], rstd[:, b, t:t + 1],
                                      ALU.subtract, ALU.mult).then_inc(z_ok, 1)

            def input_lo(b, c):
                dve.wait_ge(h_hi, DC * b + c + 1)
                dve.tensor_tensor(hT_lo[:, c, tokens(b)], hT32[:, c], hT_hi[:, c, tokens(b)].bitcast(f32),
                                  ALU.subtract).then_inc(h_lo, 1)

            def magnitude_guard(v, done):
                tmp = [guard_t[:, i] for i in range(2)]
                link(dve.tensor_scalar(tmp[0], v, -1.0, None, ALU.mult))
                link(dve.scalar_tensor_tensor(out=tmp[0], in0=tmp[0], scalar=0.25, in1=v, op0=ALU.max, op1=ALU.max))
                link(dve.tensor_scalar(tmp[1], v, 0.0, 2.0, ALU.is_ge, ALU.mult))
                dve.scalar_tensor_tensor(out=v, in0=tmp[1], scalar=-1.0, in1=tmp[0], op0=ALU.add,
                                         op1=ALU.mult).then_inc(done, 1)

            for t in range(QT):
                if t % 2 == 0:
                    dve.wait_ge((ld_x_first, ld_x[0])[t // 2], 16)
                row_statistics(0, t)
            variances(0)
            normalise(0)
            dve.wait_ge(ld_w["k"], LDW)
            wk = (codes["k"], scales["k"], w32["k"])
            dve.tensor_tensor(wk[2], wk[0], wk[1], ALU.mult).then_inc(w_prod["k"], 1)
            dve.tensor_tensor(w_hi["k"][:, :, :], wk[0], wk[1], ALU.mult).then_inc(w_hi_ok["k"], 2)
            dve.wait_ge(w_prod["k"], 1)
            dve.wait_ge(w_hi_ok["k"], 2)
            dve.tensor_tensor(w_lo["k"][:, :, :], wk[2], w_hi["k"][:, :, :].bitcast(f32), ALU.subtract).then_inc(w_ok["k"], 2)
            for c in range(DC):
                input_lo(0, c)
            dve.wait_ge(vec_tr, 1)
            dve.tensor_copy(vecT[:, NH:VECS], y_ps[:, NH:VECS]).then_inc(vec_ok, 1)
            dve.tensor_scalar(vecT[:, 0:NH], y_ps[:, 0:NH], SCORE_SCALE, None, ALU.mult).then_inc(vec_ok, 1)
            dve.wait_ge(vec_ok, 2)

            def q_low(count, head):
                dve.wait_ge(q_hi_ok, count)
                dve.scalar_tensor_tensor(out=q_lo[:, :], in0=qv_ps[:, :], scalar=bias[:, 0, head], in1=q_hi[:, :].bitcast(f32),
                                         op0=ALU.add, op1=ALU.subtract).then_inc(q_ok, 1)

            def k_low(count, head):
                dve.wait_ge(k_hi_ok, count)
                dve.scalar_tensor_tensor(out=k_lo[:, :], in0=ky_ps[:, :], scalar=bias[:, 1, head], in1=k_hi[:, :].bitcast(f32),
                                         op0=ALU.add, op1=ALU.subtract).then_inc(k_ok, 1)

            def o_low(count, head):
                dve.wait_ge(o_hi_ok, count)
                dve.scalar_tensor_tensor(out=o_lo[:, :], in0=o_ps[:, :], scalar=bias[:, 2, head], in1=o_hi[:, :].bitcast(f32),
                                         op0=ALU.add, op1=ALU.subtract).then_inc(o_ok, 1)

            def y_add(count, b, c, fresh, bank=None):
                ps = (y_ps, ky_ps)[c] if bank is None else bank
                dve.wait_ge(y_mm, count)
                if fresh:
                    dve.tensor_copy(yT[:, c, tokens(b)], ps[:, :]).then_inc(y_ok, 1)
                else:
                    dve.tensor_tensor(yT[:, c, tokens(b)], ps[:, :], yT[:, c, tokens(b)], ALU.add).then_inc(y_ok, 1)

            q_low(1, slice(0, 1))
            k_low(1, slice(0, 1))

            def head_slice(p, s):
                if s < 0:
                    h = 2 * p - 1
                elif s >= SPP:
                    h = 2 * p + 2
                else:
                    h = 2 * p + s % 2
                return bass.ds(h, 1)

            def pair(p, first=False, last=False):
                for s in range(SPP):
                    n = SPP * p + s
                    start, end = first and s == 0, last and s == SPP - 1
                    if start:
                        dve.wait_ge(ld_x[1], 16)
                        statistics(1)

                    def maximum(i):
                        dve.wait_ge(s_mm, QT * n + i + 1)
                        dve.tensor_reduce(neg_max[:, i:i + 1], score_ps[i % 2][:, :], AX.X, ALU.max,
                                          negate=True).then_inc(max_ok, 1)

                    def inverse(i):
                        dve.wait_ge(exp_ok, QT * n + i + 1)
                        dve.reciprocal(inv_sum[:, i:i + 1], row_sum[:, i:i + 1]).then_inc(inv_ok, 1)

                    def prob_low(i):
                        dve.wait_ge(p_hi_ok, QT * n + i + 1)
                        dve.tensor_tensor(pT_lo[:, s % 2, :, i * P:(i + 1) * P],
                                          tr_ps[i % 2][:, :].rearrange("p (k q) -> p k q", k=QT),
                                          pT_hi[:, s % 2, :, i * P:(i + 1) * P].bitcast(f32), ALU.subtract).then_inc(p_ok, 1)

                    new = INPUT_AT[s] if first and s in INPUT_AT else None
                    made = INPUT_AT[s - 1] if first and s - 1 in INPUT_AT else None
                    if new:
                        dve.wait_ge(ld_x[new], 16)
                    maximum(0)
                    if not (first and s < 2):
                        y_add(DC * (n - 1), batch_of(s - 2), 1, first and s % 2 == 0)
                    maximum(1)
                    if start:
                        normalise(1)
                    if new:
                        row_statistics(new, 0)
                    inverse(0)
                    maximum(2)
                    if made:
                        input_lo(made, 0)
                    if new:
                        row_statistics(new, 1)
                    inverse(1)
                    maximum(3)
                    if made:
                        input_lo(made, 1)
                    if new:
                        row_statistics(new, 2)
                        row_statistics(new, 3)
                    inverse(2)
                    if new:
                        variances(new)
                    if end:
                        dve.wait_ge(mod2_ev, 1)
                        magnitude_guard(mod_row[:, 0:D], ga_ok)
                    inverse(3)
                    if start:
                        for c in range(DC):
                            input_lo(1, c)
                    if not start:
                        o_low(n, head_slice(p, s - 1))
                    prob_low(0)
                    if not end:
                        q_low(n + 2, head_slice(p, s + 1))
                    prob_low(1)
                    if not end:
                        k_low(n + 2, head_slice(p, s + 1))
                    if end:
                        dve.wait_ge(mod_ok, 3)
                        for c in range(DC):
                            dve.tensor_scalar(ga_bo[:, c], modT[:, GA + c], bo_sb[:, c:c + 1], None, ALU.mult).then_inc(ga_bo_ok, 1)
                    prob_low(2)
                    if new:
                        normalise(new)
                    prob_low(3)
                    if not start and not end:
                        y_add(DC * (n - 1) + 1, batch_of(s - 1), 0, first and s % 2 == 1)
            pair(0, first=True)
            dve.wait_ge(y_zero, 1)
            with dve.Fori(1, PAIRS - 1) as p:
                pair(p)
            pair(PAIRS - 1, last=True)
            N = SPP * PAIRS

            def attended(b):
                for u in range(2):
                    dve.wait_ge(x1_tr, 2 * b + u + 1)
                    t = b * QT + 2 * u
                    dve.tensor_tensor(x_nat[:, t:t + 2], score_ps[u][:, :].rearrange("p (t d) -> p t d", t=2),
                                      x_nat[:, t:t + 2], ALU.add).then_inc(x1_ok, 1)
                dve.wait_ge(x1_ok, 2 * (b + 1))
                statistics(b)

            def ffn_rows(b):
                if b >= 2:
                    dve.wait_ge(z2_tr, DC * (b - 1))
                normalise(B + b)

            attended(0)
            for c in range(DC):
                y_add(DC * (N - 2) + c + 1, B - 1, c, False)
            ffn_rows(0)
            attended(1)
            o_low(N, slice(FEAT // P - 1, FEAT // P))
            ffn_rows(1)
            attended(2)
            for c in range(DC):
                y_add(DC * (N - 1) + c + 1, B - 1, c, False, (y_ps, o_ps)[c])
            ffn_rows(2)
            dve.tensor_copy(pick, ident[0:B, 0:B].unsqueeze(2).to_broadcast([B, B, P])).then_inc(pick_ok, 1)
            dve.wait_ge(ga_ok, 1)
            dve.wait_ge(mod2_ev, 2)
            at = (GB - GA) * P
            magnitude_guard(mod_row[:, at:at + D], gb_ok)
            attended(3)
            dve.wait_ge(ffn_ev, 3)
            dve.wait_ge(gbb_ok, 1)
            dve.tensor_tensor(w_gb[0], wT[:, :, :], gb_row[:, 0:1].to_broadcast([P, DC, O]), ALU.mult).then_inc(wg_ok[0], 1)
            dve.tensor_tensor(b_gb[0], bT[:, :], gb_row[:, 0], ALU.mult).then_inc(wg_ok[0], 1)
            ffn_rows(3)

            chained = [0]

            def chain(ins):
                chained[0] += 1
                ins.then_inc(router_step, 1)
                dve.wait_ge(router_step, chained[0])

            def wide(v):
                return v.unsqueeze(2).to_broadcast([P, GT, EXP])

            def first_greatest(src, most, hot):
                chain(dve.tensor_reduce(most, src[:, :, :], AX.X, ALU.max))
                chain(dve.tensor_tensor(cand[:, :, :], src[:, :, :], wide(most), ALU.is_equal))
                chain(dve.scalar_tensor_tensor(out=cand[:, :, :], in0=cand[:, :, :], scalar=-float(EXP), in1=iota8[:, :, :],
                                               op0=ALU.mult, op1=ALU.add))
                chain(dve.tensor_reduce(top[:, 7], cand[:, :, :], AX.X, ALU.min))
                chain(dve.tensor_tensor(hot[:, :, :], cand[:, :, :], wide(top[:, 7]), ALU.is_equal))

            def router(g):
                tiles = slice(g * GT, (g + 1) * GT)
                dve.wait_ge(ag_ev, GT * (g + 1))
                logits = logit[:, tiles]
                first_greatest(logits, top[:, 0], hot1)
                chain(dve.scalar_tensor_tensor(out=masked[:, :, :], in0=hot1[:, :, :], scalar=-3.0e38, in1=logits,
                                               op0=ALU.mult, op1=ALU.add))
                first_greatest(masked, top[:, 1], hot2)
                dve.tensor_tensor(top[:, 3], top[:, 1], top[:, 0], ALU.subtract).then_inc(margin_ok, 1)
                dve.wait_ge(e2_ok, g + 1)
                chain(dve.tensor_scalar(top[:, 5], top[:, 4], 1.0, None, ALU.add))
                chain(dve.reciprocal(top[:, 6], top[:, 5]))
                chain(dve.tensor_scalar(top[:, 5], top[:, 6], LORA_ALPHA, None, ALU.mult))
                chain(dve.tensor_tensor(top[:, 6], top[:, 5], top[:, 4], ALU.mult))
                chain(dve.tensor_tensor(hot1[:, :, :], hot1[:, :, :], wide(top[:, 5]), ALU.mult))
                chain(dve.tensor_tensor(hot2[:, :, :], hot2[:, :, :], wide(top[:, 6]), ALU.mult))
                dve.tensor_tensor(wmat[:, tiles], hot1[:, :, :], hot2[:, :, :], ALU.add).then_inc(wmat_ok, 1)

            dve.wait_ge(iota_ok, EXP)
            for g in range(GROUPS):
                router(g)
            for i in range(2 * B):
                dve.wait_ge(f_mm, i + 1)
                dve.tensor_tensor(x_nat[:, 2 * i:2 * i + 2], f_banks[i][:, :].rearrange("p (t d) -> p t d", t=2),
                                  x_nat[:, 2 * i:2 * i + 2], ALU.add).then_inc(res_ok, 1)

        @block.tensor
        def _(pe):
            def three(dst, a, b_, first, last):
                (a_hi, a_lo), (b_hi, b_lo) = a, b_
                pe.matmul(dst, a_hi, b_hi, start=first, stop=False)
                pe.matmul(dst, a_hi, b_lo, start=False, stop=False)
                return pe.matmul(dst, a_lo, b_hi, start=False, stop=last)

            pe.wait_ge(ident_ok, 1)
            pe.wait_ge(ld_c, 16)
            pe.transpose(o_ps[:, 0:B * DC], c_raw[:, :], ident[0:B * DC, 0:B * DC]).then_inc(c_tr, 1)
            pe.wait_ge(ld_wmod, 16)
            pe.wait_ge(silu_ok, 1)
            silu = c_silu[:, :].rearrange("p (b c) -> p c b", c=DC)
            for j in range(SA, GA):
                for c in range(DC):
                    ins = pe.matmul(ky_ps[:, j * B:(j + 1) * B], wmod_1[:, c, j * P:(j + 1) * P], silu[:, c],
                                    start=(c == 0), stop=(c == DC - 1))
            ins.then_inc(mod_mm, 1)

            def transpose_input(b, banks):
                pe.wait_ge(z_ok, QT * (b + 1))
                for c in range(DC):
                    for t in range(QT):
                        ins = pe.transpose(banks[c][:, t * P:(t + 1) * P], z[:, b % 2, t, c * P:(c + 1) * P], ident[:, :])
                    ins.then_inc(h_tr, 1)

            transpose_input(0, tr_ps)
            pe.wait_ge(ld_vec, 16 * 4)
            pe.transpose(y_ps[:, 0:VECS], vec_raw[:, :], ident[0:VECS, 0:VECS]).then_inc(vec_tr, 1)

            def project(dst, m, j, b):
                for c in range(DC):
                    cut = (slice(None), c, slice(j * HD, (j + 1) * HD))
                    ins = three(dst[:, :], (w_hi[m][cut], w_lo[m][cut]),
                                (hT_hi[:, c, tokens(b)], hT_lo[:, c, tokens(b)]), c == 0, c == DC - 1)
                return ins

            def project_v(b, half):
                for t in range(2):
                    first = b * S + (2 * half + t) * P
                    for c in range(DC):
                        cut = (slice(None), c, slice(first, first + P))
                        ins = three(qv_ps[:, t * PW:(t + 1) * PW], (hT_hi[cut], hT_lo[cut]),
                                    (w_hi["v"][:, c], w_lo["v"][:, c]), c == 0, c == DC - 1)
                return ins

            pe.wait_ge(h_lo, DC)
            pe.wait_ge(w_ok["q"], 1)
            project(qv_ps, "q", 0, 0).then_inc(q_mm, 1)
            pe.wait_ge(w_ok["k"], 1)
            pe.wait_ge(mod_ok, 2)
            project(ky_ps, "k", 0, 0).then_inc(k_mm, 1)
            pe.wait_ge(w_ok["v"], 1)
            pe.wait_ge(q_ok, 1)
            project_v(0, 0).then_inc(v_mm, 1)
            pe.wait_ge(v32_ok, 1)
            project_v(0, 1).then_inc(v_mm, 1)

            def weighted(par_step, vpar, j, kt):
                cut = (slice(None), vpar, kt, slice(j * HD, (j + 1) * HD))
                return three(o_ps[:, :], (v_hi[cut], v_lo[cut]), (pT_hi[:, par_step, kt], pT_lo[:, par_step, kt]),
                             kt == 0, kt == QT - 1)

            def out_project(c, j, bank=None):
                cut = (slice(None), j, slice(c * P, (c + 1) * P))
                bank = (y_ps, ky_ps)[c] if bank is None else bank
                return three(bank[:, :], (w_hi["o"][cut], w_lo["o"][cut]), (o_hi[:, :], o_lo[:, :]), True, True)

            def modulation_rows(i):
                pe.wait_ge(ld_wmod2, 16)
                for c in range(DC):
                    ins = pe.matmul((qv_ps, ky_ps)[i][0:B, :], silu[:, c], wmod_2[:, c, i * S:(i + 1) * S],
                                    start=(c == 0), stop=(c == DC - 1))
                ins.then_inc(mod2_mm, 1)

            def modulation_columns(ps, first, count):
                for j in range(count):
                    at = (first + j) * P
                    ins = pe.transpose(ps[:, j * B:(j + 1) * B], mod_row[:, at:at + P], ident[0:B, 0:B])
                ins.then_inc(mod2_tr, 1)

            def rows_of_y(b):
                pe.wait_ge(yg_ok[b], DC)
                for u in range(2):
                    if b:
                        pe.wait_ge(x1_ok, 2 * (b - 1) + u + 1)
                    for t in range(2):
                        for c in range(DC):
                            first = b * S + (2 * u + t) * P
                            ins = pe.transpose(score_ps[u][:, t * D + c * P:t * D + (c + 1) * P], yT[:, c, first:first + P], ident[:, :])
                    ins.then_inc(x1_tr, 1)

            def gb_everywhere(i):
                at = (GB - GA) * P
                for b in range(2):
                    ins = pe.matmul((o_ps, y_ps)[i][:, b * D:(b + 1) * D], pick[:, 2 * i + b], mod_row[:, at:at + D], start=True, stop=True)
                ins.then_inc(gbb_mm, 1)

            def ffn_dense_weights():
                pe.wait_ge(ld_ffn, 16 * (3 + O // P))
                pe.wait_ge(mod_ok, 4)
                for c in range(DC):
                    for r in range(O // P):
                        ins = pe.transpose(qv_ps[:, c * O + r * P:c * O + (r + 1) * P], w_raw[:, r, c * P:(c + 1) * P], ident[:, :])
                ins.then_inc(ffn_tr, 1)

            def pair(p, first=False, last=False):
                for s in range(SPP):
                    n = SPP * p + s
                    b = batch_of(s)
                    prev = (s - 1) % SPP
                    nxt = (s + 1) % SPP
                    start, end = first and s == 0, last and s == SPP - 1
                    early = first and s < 2
                    pe.wait_ge(q_ok, n + 1)
                    pe.wait_ge(k_ok, n + 1)
                    for i in range(QT):
                        if not (start and i < 2):
                            pe.wait_ge(exp_ok, QT * n + i - 1)
                        cut = (slice(None), slice(i * P, (i + 1) * P))
                        three(score_ps[i % 2][:, :], (q_hi[cut], q_lo[cut]), (k_hi[:, :], k_lo[:, :]),
                              True, True).then_inc(s_mm, 1)
                        if not start:
                            if i == 0:
                                pe.wait_ge(p_ok, QT * n)
                                if first and s == 1:
                                    pe.wait_ge(h_hi, DC * 2)
                                pe.wait_ge(v_ok, n + s % 2)
                                if not early:
                                    pe.wait_ge(o_ok, n - 1)
                            ins = weighted((s - 1) % 2, batch_of(prev) % 2, prev % 2, i)
                            if i == QT - 1:
                                ins.then_inc(o_mm, 1)
                    if start:
                        pe.wait_ge(vec_ok, 2)
                        transpose_input(1, (o_ps, y_ps))

                    def transpose_probs(i):
                        pe.wait_ge(prob_ok, QT * n + i + 1)
                        if first and s - 1 in INPUT_AT and i < DC:
                            pe.wait_ge(h_hi, DC * INPUT_AT[s - 1] + i + 1)
                        if not (start and i < 2):
                            pe.wait_ge(p_ok, QT * n + i - 1)
                        for kt in range(QT):
                            ins = pe.transpose(tr_ps[i % 2][:, kt * P:(kt + 1) * P], prob[:, i, kt * P:(kt + 1) * P], ident[:, :])
                        ins.then_inc(p_tr, 1)

                    transpose_probs(0)
                    if not end:
                        if first:
                            pe.wait_ge(h_lo, DC * (batch_of(nxt) + 1 if nxt else B))
                        if s >= SPP - 1 or s == 0:
                            pe.wait_ge(w_ok["q"], 2 * p + (3 if s else 2))
                        pe.wait_ge(v32_ok, n + 2)
                        project(qv_ps, "q", nxt % 2, batch_of(nxt)).then_inc(q_mm, 1)
                    if end:
                        pe.wait_ge(y_ok, DC * (n - 1))
                        modulation_rows(1)
                    transpose_probs(1)
                    if not end:
                        if s >= SPP - 1 or s == 0:
                            pe.wait_ge(w_ok["k"], 2 * p + (3 if s else 2))
                        if not early:
                            pe.wait_ge(y_ok, DC * (n - 1))
                        project(ky_ps, "k", nxt % 2, batch_of(nxt)).then_inc(k_mm, 1)
                    if end:
                        pe.wait_ge(ga_ok, 1)
                        modulation_columns(qv_ps, 0, CB - GA)
                    transpose_probs(2)
                    if end:
                        pe.wait_ge(mod2_ev, 2)
                        modulation_columns(ky_ps, CB - GA, GB - CB)
                    if last and s == SPP - 2:
                        pe.wait_ge(q_ok, n + 2)
                        modulation_rows(0)
                    if not (last and s >= SPP - SPB):
                        if first:
                            pe.wait_ge(h_lo, DC * min(b + 2, B))
                        if s == SPP - SPB:
                            pe.wait_ge(w_ok["v"], p + 2)
                        pe.wait_ge(q_ok, n + 2)
                        project_v((b + 1) % B, s % 2).then_inc(v_mm, 1)
                    transpose_probs(3)
                    if not start:
                        pe.wait_ge(o_ok, n)
                        if s == 1 or s == 2:
                            pe.wait_ge(w_ok["o"], 2 * p + s)
                        if not early:
                            pe.wait_ge(y_ok, DC * (n - 1) - 1)
                        out_project(0, prev % 2).then_inc(y_mm, 1)
                        if not end:
                            pe.wait_ge(k_ok, n + 2)
                        else:
                            pe.wait_ge(mod_ok, 5)
                        out_project(1, prev % 2).then_inc(y_mm, 1)
                        if end:
                            ffn_dense_weights()
                            rows_of_y(0)
                    if first and s in INPUT_AT:
                        pe.wait_ge(p_ok, QT * (n + 1))
                        transpose_input(INPUT_AT[s], tr_ps)

            pair(0, first=True)
            with pe.Fori(1, PAIRS - 1) as p:
                pair(p)
            pair(PAIRS - 1, last=True)

            N = SPP * PAIRS
            pe.wait_ge(p_ok, QT * N)
            pe.wait_ge(o_ok, N - 1)
            for kt in range(QT):
                ins = weighted((N - 1) % 2, (B - 1) % 2, 1, kt)
            ins.then_inc(o_mm, 1)

            def ffn_input(b):
                pe.wait_ge(z_ok, QT * (B + b + 1))
                for c in range(DC):
                    if b:
                        pe.wait_ge(z2_ev, DC * (b - 1) + c + 1)
                    for t in range(QT):
                        ins = pe.transpose(tr_ps[c][:, t * P:(t + 1) * P], z[:, b % 2, t, c * P:(c + 1) * P], ident[:, :])
                    ins.then_inc(z2_tr, 1)

            def lora_rows(b):
                pe.wait_ge(z2_ev, DC * (b + 1))
                for t in range(QT):
                    if b and t % 2 == 0:
                        pe.wait_ge(ag_ev, 4 * (b - 1) + t + 2)
                    for c in range(DC):
                        ins = pe.matmul(ag_view(t // 2)[:, t % 2], h2T[b][:, c, t * P:(t + 1) * P], agT[:, c],
                                        start=(c == 0), stop=(c == DC - 1))
                    if t % 2:
                        ins.then_inc(ag_mm, 1)

            def dense_tile(b, k):
                dst = f_banks[2 * b + k // 2][:, (k % 2) * D:(k % 2 + 1) * D]
                for c in range(DC):
                    pe.matmul(dst, h2T[b][:, c, k * P:(k + 1) * P], w_gb[b][:, c], start=(c == 0), stop=False)
                return dst

            def dense(b):
                pe.wait_ge(wg_ok[b], 2)
                for k in range(0, QT, 2):
                    dense_tile(b, k)

            def lora_transpose(b):
                pe.wait_ge(hw_ok, b + 1)
                for t in range(QT):
                    ins = pe.transpose(hwT_bank(b)[:, t * P:(t + 1) * P], lora[:, b * QT + t], ident[:, :])
                ins.then_inc(hw_tr, 1)

            def lora_add(b):
                pe.wait_ge(hwT_ok, b + 1)
                for k in range(QT):
                    if k % 2:
                        dst = dense_tile(b, k)
                    else:
                        dst = f_banks[2 * b + k // 2][:, 0:D]
                    ins = pe.matmul(dst, hwT[b][:, k * P:(k + 1) * P], b_gb[b], start=False, stop=True)
                    if k % 2:
                        ins.then_inc(f_mm, 1)

            pe.wait_ge(ffn_ev, 1)
            for c in range(DC):
                at = c * (ER + EXP)
                pe.transpose(qv_ps[:, at:at + ER], a_raw[:, c * P:(c + 1) * P], ident[:, :])
                pe.transpose(qv_ps[:, at + ER:at + ER + EXP], g_raw[:, c * P:(c + 1) * P], ident[0:EXP, 0:EXP])
            for r in range(O // P):
                ins = pe.transpose(tr_ps[0][:, r * P:(r + 1) * P], b_raw[:, r].rearrange("p e r -> p (e r)"), ident[:, :])
            ins.then_inc(ffn_tr, 1)
            rows_of_y(1)
            pe.wait_ge(ffn_ev, 3)
            ffn_input(0)
            rows_of_y(2)
            pe.wait_ge(y_ok, DC * (N - 1))
            lora_rows(0)
            ffn_input(1)
            pe.wait_ge(o_ok, N)
            for c in range(DC):
                out_project(c, 1, (y_ps, o_ps)[c]).then_inc(y_mm, 1)
            lora_rows(1)
            ffn_input(2)
            rows_of_y(3)
            pe.wait_ge(gb_ok, 1)
            pe.wait_ge(pick_ok, 1)
            pe.wait_ge(y_ok, DC * N)
            gb_everywhere(0)
            gb_everywhere(1)
            lora_rows(2)
            pe.wait_ge(gbb_ok, 2)
            dense(0)
            ffn_input(3)
            pe.wait_ge(x1_ok, 2 * B)
            dense(1)
            lora_rows(3)
            pe.wait_ge(ag_ev, 4 * B)
            dense(2)
            lora_transpose(0)
            lora_transpose(1)
            lora_add(0)
            lora_add(1)
            dense(3)
            for b in (2, 3):
                pe.wait_ge(res_ok, b - 1)
                lora_transpose(b)
            lora_add(2)
            lora_add(3)


_INS = ["L0_attn_x", "L0_attn_wq_codes", "L0_attn_wq_scales", "L0_attn_bq", "L0_attn_wk_codes", "L0_attn_wk_scales",
        "L0_attn_bk", "L0_attn_wv_codes", "L0_attn_wv_scales", "L0_attn_bv", "L0_attn_wo_codes", "L0_attn_wo_scales",
        "L0_attn_bo", "L0_ffn_W", "L0_ffn_gate_w", "L0_ffn_A", "L0_ffn_B", "L0_c", "L0_wmod"]
_OUTS = [((4, 512, 256), "float32")]


def kernel(**inputs):
    import numpy as _np
    import concourse.bacc as _bacc
    from concourse import mybir as _mybir
    from concourse.bass_utils import run_bass_kernel_spmd as _run

    nc = _bacc.Bacc("TRN2", target_bir_lowering=False, num_devices=1)
    arrays, args = {}, []
    for name in _INS:
        a = _np.ascontiguousarray(inputs[name])
        arrays[f"in_{name}_dram"] = a
        args.append(nc.dram_tensor(f"in_{name}_dram", a.shape, _mybir.dt.from_np(a.dtype), kind="ExternalInput").ap())
    for i, (shape, dtype) in enumerate(_OUTS):
        dt = _mybir.dt.from_np(_np.dtype(dtype))
        args.append(nc.dram_tensor(f"out_{i}_dram", shape, dt, kind="ExternalOutput").ap())
    bass_adaln_mxfp4_attention_moe_lora_kernel(nc, *args)
    r = _run(nc, [arrays], core_ids=[0])
    got = tuple(r.results[0][f"out_{i}_dram"] for i in range(len(_OUTS)))
    return got[0]
```
